# Optimizing a Trainium2 kernel written in Bass

```python
import numpy as np
import jax
import jax.numpy as jnp

def _softmax(x, axis=-1):
    return jax.nn.softmax(x, axis=axis)

def _gelu(x):
    return jax.nn.gelu(x, approximate=True)

def _silu(x):
    return jax.nn.silu(x)

def _sigmoid(x):
    return jax.nn.sigmoid(x)

def _layernorm(x, axis=-1, eps=1e-05):
    m = jnp.mean(x, axis=axis, keepdims=True)
    v = jnp.var(x, axis=axis, keepdims=True)
    return (x - m) / jnp.sqrt(v + eps)

def _scatter_add(tgt, idx, src, axis=0):
    return tgt.at[idx].add(src)

def _segment_sum(src, seg, n):
    return jax.ops.segment_sum(src, seg, n)
kernel_name = 'mk_adj_resnorm_d2_adj_r2_ab6372'

def setup_inputs(seed: int=0):
    np.random.seed(seed)
    _w = jnp.asarray

    def _rec_inputs():
        import jax
        import jax.numpy as jnp
        _gk = jax.random.key(seed)
        x = 7.22e-05 + 1 * jax.random.normal(jax.random.fold_in(_gk, 1), (16, 512, 256), jnp.float32)
        _a = jax.random.bernoulli(jax.random.fold_in(_gk, 2), 0.015625, (16, 512, 512))
        _a = jnp.logical_or(_a, jnp.swapaxes(_a, -1, -2))
        _a = jnp.logical_or(_a, jnp.eye(512, dtype=bool))
        _af = _a.astype(jnp.float32)
        _af = _af * jax.random.uniform(jax.random.fold_in(_gk, 3), (16, 512, 512), jnp.float32, 0.05, 1)
        adj = _af
        _nm = jnp.ones((16, 512), dtype=bool)
        nodemask = jnp.where(_nm, 1.0, 0.0).astype(jnp.float32)
        return (x, adj, nodemask)
    x, adj, nodemask = _rec_inputs()

    def _L0_gnn_setup():
        import jax, jax.numpy as jnp
        import numpy as np
        EPS_LN = 1e-05

        def hypergraph_conv(x, adj, W, b):
            N, C, _ = adj.shape
            H = (adj != 0).astype(x.dtype)
            w = adj.reshape(N, -1)[:, :C]
            xw = jnp.einsum('ncd,hd->nch', x, W)
            Dn = jnp.einsum('nce,ne->nc', H, w)
            Dn = jnp.where(Dn > 0, 1.0 / Dn, 0.0)
            Be = H.sum(axis=1)
            Be = jnp.where(Be > 0, 1.0 / Be, 0.0)
            m = Be[:, :, None] * jnp.einsum('nce,nch->neh', H, xw)
            out = Dn[:, :, None] * jnp.einsum('nce,neh->nch', H, m)
            return out + b

        def layer_norm(x, g, b):
            mu = jnp.mean(x, axis=-1, keepdims=True)
            var = jnp.var(x, axis=-1, keepdims=True)
            return (x - mu) * jax.lax.rsqrt(var + EPS_LN) * g + b
        key = jax.random.key(seed)
        ks = jax.random.split(key, 4)
        N, C, Din, Dh, Dout = (16, 512, 256, 512, 256)
        x = jax.random.normal(ks[0], (N, C, Din), dtype=jnp.float32)
        adj = jax.random.uniform(ks[1], (N, C, C), dtype=jnp.float32, minval=0.1, maxval=1.0)
        W1 = jax.random.normal(ks[2], (Dh, Din), dtype=jnp.float32) * (1.0 / np.sqrt(Din))
        b1 = jnp.zeros((Dh,), dtype=jnp.float32)
        gamma = jnp.ones((Dh,), dtype=jnp.float32)
        beta = jnp.zeros((Dh,), dtype=jnp.float32)
        W2 = jax.random.normal(ks[3], (Dout, Dh), dtype=jnp.float32) * (1.0 / np.sqrt(Dh))
        b2 = jnp.zeros((Dout,), dtype=jnp.float32)
        return {'x': x, 'adj': adj, 'W1': W1, 'b1': b1, 'gamma': gamma, 'beta': beta, 'W2': W2, 'b2': b2}
    _L0_gnn_all = _L0_gnn_setup()
    _L0_gnn_in = {k: v for k, v in _L0_gnn_all.items() if k in ('W1', 'b1', 'gamma', 'beta', 'W2', 'b2')}
    del _L0_gnn_all

    def _L1_gnn_setup():
        import jax, jax.numpy as jnp
        import numpy as np
        B, N, IN_DIM, ATT_DIM = (2, 4096, 256, 256)
        key = jax.random.key(seed)
        k1, k2, k3, k4 = jax.random.split(key, 4)
        X = jax.random.normal(k1, (B, N, IN_DIM), dtype=jnp.float32)
        adj = jax.random.uniform(k2, (B, N, N), dtype=jnp.float32)
        mask = jnp.ones((B, N), dtype=jnp.float32)
        Wqk = jax.random.normal(k3, (IN_DIM, 2 * ATT_DIM), dtype=jnp.float32) / np.sqrt(IN_DIM)
        Wv = jax.random.normal(k4, (IN_DIM, IN_DIM), dtype=jnp.float32) / np.sqrt(IN_DIM)
        return {'X': X, 'adj': adj, 'mask': mask, 'Wqk': Wqk, 'Wv': Wv}
    _L1_gnn_all = _L1_gnn_setup()
    _L1_gnn_in = {k: v for k, v in _L1_gnn_all.items() if k in ('Wqk', 'Wv')}
    del _L1_gnn_all
    return {'x': x, 'adj': adj, 'nodemask': nodemask, 'L0_gnn_W1': _L0_gnn_in['W1'], 'L0_gnn_b1': _L0_gnn_in['b1'], 'L0_gnn_gamma': _L0_gnn_in['gamma'], 'L0_gnn_beta': _L0_gnn_in['beta'], 'L0_gnn_W2': _L0_gnn_in['W2'], 'L0_gnn_b2': _L0_gnn_in['b2'], 'L1_gnn_Wqk': _L1_gnn_in['Wqk'], 'L1_gnn_Wv': _L1_gnn_in['Wv']}

def reference(x, adj, nodemask, L0_gnn_W1, L0_gnn_b1, L0_gnn_gamma, L0_gnn_beta, L0_gnn_W2, L0_gnn_b2, L1_gnn_Wqk, L1_gnn_Wv):
    import jax
    import jax.numpy as jnp

    def _L0_gnn_ref(x, adj, W1, b1, gamma, beta, W2, b2):
        import jax, jax.numpy as jnp
        import numpy as np
        EPS_LN = 1e-05

        def hypergraph_conv(x, adj, W, b):
            N, C, _ = adj.shape
            H = (adj != 0).astype(x.dtype)
            w = adj.reshape(N, -1)[:, :C]
            xw = jnp.einsum('ncd,hd->nch', x, W)
            Dn = jnp.einsum('nce,ne->nc', H, w)
            Dn = jnp.where(Dn > 0, 1.0 / Dn, 0.0)
            Be = H.sum(axis=1)
            Be = jnp.where(Be > 0, 1.0 / Be, 0.0)
            m = Be[:, :, None] * jnp.einsum('nce,nch->neh', H, xw)
            out = Dn[:, :, None] * jnp.einsum('nce,neh->nch', H, m)
            return out + b

        def layer_norm(x, g, b):
            mu = jnp.mean(x, axis=-1, keepdims=True)
            var = jnp.var(x, axis=-1, keepdims=True)
            return (x - mu) * jax.lax.rsqrt(var + EPS_LN) * g + b
        h = jax.nn.relu(hypergraph_conv(x, adj, W1, b1))
        h = layer_norm(h, gamma, beta)
        y = hypergraph_conv(h, adj, W2, b2)
        return y + x

    def _L1_gnn_ref(X, adj, mask, Wqk, Wv):
        import jax, jax.numpy as jnp
        import numpy as np
        B, N, IN_DIM, ATT_DIM = (2, 4096, 256, 256)
        qk = X @ Wqk
        q, k = jnp.split(qk, 2, axis=-1)
        v = X @ Wv
        att_dim = q.shape[-1]
        inv_scale = 1.0 / jnp.sqrt(jnp.float32(att_dim))
        k_m = k * mask[:, :, None]
        agg = jnp.einsum('bij,bjd->bid', adj, k_m)
        w = inv_scale * mask * jnp.einsum('bid,bid->bi', q, agg)
        L = jax.nn.softmax(w, axis=1)[:, :, None] * v
        return L
    x = _layernorm(x + _L0_gnn_ref(x, adj, L0_gnn_W1, L0_gnn_b1, L0_gnn_gamma, L0_gnn_beta, L0_gnn_W2, L0_gnn_b2), axis=-1)
    x = _layernorm(x + _L1_gnn_ref(x, adj, nodemask, L1_gnn_Wqk, L1_gnn_Wv), axis=-1)
    return x

_drawn_inputs = setup_inputs


def setup_inputs(seed=0):
    import zlib

    import numpy as np

    out = dict(_drawn_inputs(seed))
    spreads = {'L0_gnn_b1': (0.0, 0.1),
     'L0_gnn_gamma': (1.0, 0.2),
     'L0_gnn_beta': (0.0, 0.1),
     'L0_gnn_b2': (0.0, 0.1)}
    factors = {}
    for name, (base, spread) in spreads.items():
        noise = np.random.default_rng([zlib.crc32(name.encode()), seed]).standard_normal(out[name].shape)
        drawn = base * np.exp(spread * noise) if base else spread * noise
        out[name] = jnp.asarray(drawn.astype(out[name].dtype))
    for name, factor in factors.items():
        out[name] = (out[name] * factor).astype(out[name].dtype)
    return out
```

```python
from contextlib import ExitStack

import concourse.bass as bass
from concourse import mybir

P = 128
F32 = mybir.dt.float32
F32R = mybir.dt.float32r
BF16 = mybir.dt.bfloat16
ALU = mybir.AluOpType
ACT = mybir.ActivationFunctionType
AX_X = mybir.AxisListType.X
EPS = 1e-5
TINY = 1.17549435e-38



def graph_kernel(nc, x, adj, nodemask, W1, b1, gamma, beta, W2, b2, Wqk, Wv, out):
    B, N, D = x.shape
    HID = W1.shape[0]
    NB = N // P
    DB = D // P
    HB = HID // P
    BANK = 512
    assert NB == 4 and DB == 2 and HB == 4 and N == BANK and HID == BANK and Wqk.shape[1] == 2 * D
    SCALE = float(D) ** -0.5

    with ExitStack() as ctx:
        def sb(name, shape, dt=F32):
            return ctx.enter_context(nc.sbuf_tensor(name, shape, dt))

        def sem(name):
            return ctx.enter_context(nc.semaphore(name))

        bank = [ctx.enter_context(nc.psum_tensor(f"bank{i}", [P, BANK], F32)) for i in range(8)]

        HT_bank = [bank[6 + h][:, :].bitcast(BF16) for h in range(2)]

        adj_raw = [sb(f"adj_raw{q}", [P, NB, N]) for q in range(2)]
        adj_masked = [sb(f"adj_masked{q}", [P, NB, N]) for q in range(2)]
        x_raw = [sb(f"x_raw{q}", [P, NB, D]) for q in range(2)]
        H = [sb(f"H{q}", [P, NB, N], F32R) for q in range(2)]
        H_bf = sb("H_bf", [P, NB, N], BF16)
        HT = [sb(f"HT{q}", [P, NB, N], F32R) for q in range(2)]
        row0 = [sb(f"row0_{q}", [P, N]) for q in range(2)]
        maskrow = [sb(f"maskrow{q}", [P, N]) for q in range(2)]
        count = [sb(f"count{q}", [P, NB]) for q in range(2)]
        Be = [sb(f"Be{q}", [P, NB]) for q in range(2)]
        Dn = [sb(f"Dn{q}", [P, NB]) for q in range(2)]
        x_hi = sb("x_hi", [P, NB, D], F32R)
        x_lo = sb("x_lo", [P, NB, D], F32R)
        base = sb("base", [P, NB, D])
        wide = sb("wide", [P, 2, NB, N], F32R)
        m1_hi, m1_lo = wide[:, 0, 0:2, :], wide[:, 0, 2:4, :]
        m2_hi, m2_lo = wide[:, 1, 0:2, :], wide[:, 1, 2:4, :]
        n1T_hi, n1T_lo = wide[:, 0], wide[:, 1]
        gy = sb("gy", [P, 2, 2, BANK], F32R)
        gy_hi, gy_lo = gy[:, 0], gy[:, 1]
        z = sb("z", [P, NB, HID])
        y1 = sb("y1", [P, 2, BANK])
        y2 = sb("y2", [P, NB, D])
        x1 = sb("x1", [P, NB, D])
        x1T_hi = sb("x1T_hi", [P, DB, N], F32R)
        x1T_lo = sb("x1T_lo", [P, DB, N], F32R)
        xmT_hi = sb("xmT_hi", [P, DB, N], F32R)
        xmT_lo = sb("xmT_lo", [P, DB, N], F32R)
        v = sb("v", [P, 2, BANK])
        result = sb("result", [P, NB, D])
        unused = sb("unused", [P, NB, N])
        exps, p_row = sb("exps", [1, N]), sb("p_row", [1, N])
        degree = sb("degree", [P, NB])
        inv_count, inv_degree = sb("inv_count", [P, NB]), sb("inv_degree", [P, NB])
        stats = [sb(f"stats{n}", [P, 4, 6]) for n in range(3)]
        moments = [sb(f"moments{n}", [P, 4, 2]) for n in range(3)]
        varp = [sb(f"varp{n}", [P, 4]) for n in range(3)]
        rstd = [sb(f"rstd{n}", [P, 4]) for n in range(3)]
        shift = [sb(f"shift{n}", [P, 4]) for n in range(3)]
        minus_half, eps_col = sb("minus_half", [P, 4]), sb("eps_col", [P, 4])
        w_sum, w_masked, p_col = sb("w_sum", [P, NB]), sb("w_masked", [P, NB]), sb("p_col", [P, NB])
        w_max, w_bias = sb("w_max", [1, 1]), sb("w_bias", [1, 1])
        exp_sum, exp_inv = sb("exp_sum", [1, 1]), sb("exp_inv", [1, 1])
        ident, ident_bf, ones = sb("ident", [P, P]), sb("ident_bf", [P, P], BF16), sb("ones", [P, P])
        mask_col = sb("mask_col", [P, B, NB])
        b1_row, b2_row = sb("b1_row", [P, HID]), sb("b2_row", [P, D])
        gamma_col, beta_col = sb("gamma_col", [P, HB]), sb("beta_col", [P, HB])
        W1T_hi, W1T_lo = sb("W1T_hi", [P, DB, HID], F32R), sb("W1T_lo", [P, DB, HID], F32R)
        W2T_hi, W2T_lo = sb("W2T_hi", [P, HB, D], F32R), sb("W2T_lo", [P, HB, D], F32R)
        M_hi, M_lo = sb("M_hi", [P, DB, D], F32R), sb("M_lo", [P, DB, D], F32R)
        Wv_hi, Wv_lo = sb("Wv_hi", [P, DB, D], F32R), sb("Wv_lo", [P, DB, D], F32R)
        w2beta = sb("w2beta", [P, 2, D])
        W1_in = adj_masked[0][:, 0:2, :].rearrange("p a n -> p (a n)").rearrange("p (k d) -> p k d", d=D)
        W2_in = adj_masked[0][:, 2:4, :]
        Wqk_in = adj_masked[1][:, 0:2, :]
        Wv_in = adj_masked[1][:, 2, :].rearrange("p (k d) -> p k d", d=D)
        W2T_f = z[:, 0:2, :].rearrange("p a n -> p (a n)").rearrange("p (k d) -> p k d", d=D)
        WqkT_f = z[:, 2:4, :].rearrange("p a n -> p (a n)").rearrange("p (k d) -> p k d", d=D)
        beta_wide = y1[:, :, :].rearrange("p a n -> p (a n)")[:, 0:HB * P].rearrange("p (k n) -> p k n", n=P)

        adj_in = [sem(f"adj_in{q}") for q in range(2)]
        x_in = [sem(f"x_in{q}") for q in range(2)]
        row0_in = [sem(f"row0_in{q}") for q in range(2)]
        maskrow_in = [sem(f"maskrow_in{q}") for q in range(2)]
        W1_loaded, W2_loaded, Wqk_loaded = sem("W1_loaded"), sem("W2_loaded"), sem("Wqk_loaded")
        Wv_loaded, columns_loaded, rows_loaded = sem("Wv_loaded"), sem("columns_loaded"), sem("rows_loaded")
        stored = sem("stored")
        HT_filled, m1_filled, m2_filled, g_filled = sem("HT_filled"), sem("m1_filled"), sem("m2_filled"), sem("g_filled")
        y2_filled, z_filled, x1T_filled = sem("y2_filled"), sem("z_filled"), sem("x1T_filled")
        xmT_filled, v_filled, n1T_filled = sem("xmT_filled"), sem("v_filled"), sem("n1T_filled")
        S_filled, y1_filled, w_filled, p_filled = sem("S_filled"), sem("y1_filled"), sem("w_filled"), sem("p_filled")
        x_hi_ready, m1_hi_ready, m2_hi_ready, g_hi_ready = sem("x_hi_ready"), sem("m1_hi_ready"), sem("m2_hi_ready"), sem("g_hi_ready")
        relu_ready, x1_ready, HT_ready = sem("relu_ready"), sem("x1_ready"), sem("HT_ready")
        x1T_hi_ready, xmT_hi_ready, v_ready = sem("x1T_hi_ready"), sem("xmT_hi_ready"), sem("v_ready")
        n1_ready, n1T_hi_ready, exp_ready = sem("n1_ready"), sem("n1T_hi_ready"), sem("exp_ready")
        y1_hi_ready, result_ready = sem("y1_hi_ready"), sem("result_ready")
        H_ready, H_bf_ready, Be_ready, Dn_ready = sem("H_ready"), sem("H_bf_ready"), sem("Be_ready"), sem("Dn_ready")
        m1_lo_ready, m2_lo_ready, g_lo_ready = sem("m1_lo_ready"), sem("m2_lo_ready"), sem("g_lo_ready")
        y2_ready, z_ready, x1T_lo_ready = sem("y2_ready"), sem("z_ready"), sem("x1T_lo_ready")
        xmT_lo_ready, n1T_lo_ready, scored = sem("xmT_lo_ready"), sem("n1T_lo_ready"), sem("scored")
        w_ready, y1_ready, bias_ready = sem("w_ready"), sem("y1_ready"), sem("bias_ready")
        exp_inv_ready, p_row_ready, p_ready, y3_ready = sem("exp_inv_ready"), sem("p_row_ready"), sem("p_ready"), sem("y3_ready")
        x1_end_ready, n1_end_ready, result_end_ready = sem("x1_end_ready"), sem("n1_end_ready"), sem("result_end_ready")
        max_ready, degree_ready = sem("max_ready"), sem("degree_ready")
        count_inv_ready, degree_inv_ready = sem("count_inv_ready"), sem("degree_inv_ready")
        stats_ready = [sem(f"stats_ready{n}") for n in range(3)]
        moments_ready = [sem(f"moments_ready{n}") for n in range(3)]
        shift_ready = [sem(f"shift_ready{n}") for n in range(3)]
        x_lo_ready, y1_lo_ready, masked_ready = sem("x_lo_ready"), sem("y1_lo_ready"), sem("masked_ready")
        base_ready, twice_ready = sem("base_ready"), sem("twice_ready")
        varp_ready = [sem(f"varp_ready{n}") for n in range(3)]
        rstd_ready = [sem(f"rstd_ready{n}") for n in range(3)]
        ident_zero, ident_ready, ident_bf_ready, half_ready, ones_ready = sem("ident_zero"), sem("ident_ready"), sem("ident_bf_ready"), sem("half_ready"), sem("ones_ready")
        beta_ready, W1T_filled, W2T_filled = sem("beta_ready"), sem("W1T_filled"), sem("W2T_filled")
        WqkT_filled, w2beta_filled, M_filled = sem("WqkT_filled"), sem("w2beta_filled"), sem("M_filled")
        W1T_hi_ready, W2T_hi_ready, W2T_f_ready, WqkT_f_ready = sem("W1T_hi_ready"), sem("W2T_hi_ready"), sem("W2T_f_ready"), sem("WqkT_f_ready")
        M_hi_ready, Wv_hi_ready, w2beta_ready = sem("M_hi_ready"), sem("Wv_hi_ready"), sem("w2beta_ready")
        W1T_lo_ready, W2T_lo_ready, M_lo_ready, Wv_lo_ready = sem("W1T_lo_ready"), sem("W2T_lo_ready"), sem("M_lo_ready"), sem("Wv_lo_ready")

        block = ctx.enter_context(nc.Block())

        def cols(k, n=P):
            return slice(k * n, (k + 1) * n)

        def halves(bank_ap):
            return bank_ap.rearrange("p (k d) -> p k d", d=D)

        def steps(engine, step):
            step(0, 0, 0, True, True, False)
            step(1, 1, 0, True, True, True)
            with engine.Fori(1, B // 2 - 1) as t:
                step(2 * t, 0, t, True, True, True)
                step(2 * t + 1, 1, t, True, True, True)
            step(B - 2, 0, B // 2 - 1, True, True, True)
            step(B - 1, 1, B // 2 - 1, False, True, True)
            step(B, 0, B // 2, False, False, True)

        x_dram = x.rearrange("b (p k) d -> b p k d", k=NB)
        adj_dram = adj.rearrange("b (p k) e -> b p k e", k=NB)
        adj_rows, mask_rows = adj, nodemask.rearrange("b (a n) -> b a n", a=1)
        out_dram = out.rearrange("b (p k) d -> b p k d", k=NB)

        @block.sync
        def _(sp):
            def load(b, q):
                sp.dma_start(adj_raw[q][:, :, :], adj_dram[b]).then_inc(adj_in[q], 16)
                sp.dma_start(x_raw[q][:, :, :], x_dram[b]).then_inc(x_in[q], 16)
                sp.dma_start(row0[q][:, :], adj_rows[b, 0:1, :].to_broadcast([P, N])).then_inc(row0_in[q], 16)
                sp.dma_start(maskrow[q][:, :], mask_rows[b].to_broadcast([P, N])).then_inc(maskrow_in[q], 16)

            load(0, 0)
            sp.dma_start(W1_in, W1.rearrange("(k p) d -> p k d", p=P)).then_inc(W1_loaded, 16)
            sp.dma_start(W2_in, W2.rearrange("(k p) h -> p k h", p=P)).then_inc(W2_loaded, 16)
            sp.dma_start(Wqk_in, Wqk.rearrange("(k p) a -> p k a", p=P)).then_inc(Wqk_loaded, 16)
            sp.dma_start(Wv_in, Wv.rearrange("(k p) d -> p k d", p=P)).then_inc(Wv_loaded, 16)
            with nc.allow_non_contiguous_dma(reason="two columns of 512 numbers, once"):
                sp.dma_start(gamma_col[:, :], gamma.rearrange("(k p) -> p k", p=P)).then_inc(columns_loaded, 16)
                sp.dma_start(beta_col[:, :], beta.rearrange("(k p) -> p k", p=P)).then_inc(columns_loaded, 16)
            sp.dma_start(b1_row[:, :], b1.rearrange("(a h) -> a h", a=1).to_broadcast([P, HID])).then_inc(rows_loaded, 16)
            sp.dma_start(b2_row[:, :], b2.rearrange("(a d) -> a d", a=1).to_broadcast([P, D])).then_inc(rows_loaded, 16)
            sp.dma_start(mask_col[:, :, :], nodemask.rearrange("b (p k) -> p b k", k=NB)).then_inc(rows_loaded, 16)
            load(1, 1)

            def step(i, q, half, prepare, head, tail):
                if prepare and not (isinstance(i, int) and i + 2 >= B):
                    sp.wait_ge(H_ready, i + 1)
                    sp.wait_ge(H_bf_ready, NB * i + NB)
                    sp.wait_ge(degree_ready, NB * i + NB)
                    sp.wait_ge(masked_ready, NB * i + NB)
                    sp.wait_ge(x_hi_ready, i + 1)
                    sp.wait_ge(x_lo_ready, i + 1)
                    sp.wait_ge(base_ready, i + 1)
                    load(i + 2, q)
                if tail:
                    sp.wait_ge(result_ready, i)
                    sp.wait_ge(result_end_ready, i)
                    sp.dma_start(out_dram[i - 1], result[:, :, :]).then_inc(stored, 16)

            steps(sp, step)
            sp.wait_ge(stored, 16 * B)

        @block.tensor
        def _(pe):
            def transpose_H(h):
                for k in range(2):
                    for c in range(NB):
                        last = pe.transpose(HT_bank[h][:, cols(NB * k + c)], H_bf[:, c, cols(2 * h + k)], ident_bf[:, :])
                last.then_inc(HT_filled, 1)

            def gather_edges(q, hi, lo, banks, filled):
                for k in range(NB):
                    for c in range(NB):
                        for part in (hi, lo):
                            last = pe.matmul(bank[banks[k // 2]][:, cols(k % 2, D)], H[q][:, c, cols(k)], part[:, c, :],
                                             start=(c == 0 and part is hi), stop=(c == NB - 1 and part is lo))
                    if k % 2:
                        last.then_inc(filled, 1)

            def make_m1(n, q):
                pe.wait_ge(H_ready, n + 1)
                pe.wait_ge(x_hi_ready, n + 1)
                pe.wait_ge(x_lo_ready, n + 1)
                gather_edges(q, x_hi, x_lo, (0, 1), m1_filled)

            pe.wait_ge(ident_ready, 1)
            pe.wait_ge(ident_bf_ready, 1)
            pe.wait_ge(H_bf_ready, NB)
            transpose_H(0)
            transpose_H(1)
            pe.wait_ge(W1_loaded, 16)
            for d in range(DB):
                for k in range(HB):
                    last = pe.transpose(bank[2 + d][:, cols(k)], W1_in[:, k, cols(d)], ident[:, :])
                last.then_inc(W1T_filled, 1)
            pe.wait_ge(W2_loaded, 16)
            for k in range(HB):
                for d in range(DB):
                    last = pe.transpose(bank[4 + k // 2][:, (k % 2) * D + d * P:(k % 2) * D + (d + 1) * P],
                                        W2_in[:, d, cols(k)], ident[:, :])
                if k % 2:
                    last.then_inc(W2T_filled, 1)
            make_m1(0, 0)
            pe.wait_ge(HT_ready, NB)
            pe.wait_ge(Wqk_loaded, 16)
            for k in range(4):
                for d in range(DB):
                    last = pe.transpose(bank[6 + k // 2][:, (k % 2) * D + d * P:(k % 2) * D + (d + 1) * P],
                                        Wqk_in[:, d, cols(k)], ident[:, :])
                if k % 2:
                    last.then_inc(WqkT_filled, 1)
            pe.wait_ge(WqkT_f_ready, 2)
            pe.wait_ge(W1T_lo_ready, 2)
            for d in range(DB):
                for a in range(2):
                    last = pe.matmul(bank[3][:, cols(d, D)], WqkT_f[:, a, cols(d)], WqkT_f[:, 2 + a, :],
                                     start=(a == 0), stop=(a == 1))
            last.then_inc(M_filled, 1)
            pe.wait_ge(W2T_f_ready, 2)
            pe.wait_ge(beta_ready, 1)
            for k in range(HB):
                last = pe.matmul(bank[2][:, 0:D], beta_wide[:, k, :], W2T_f[:, k, :],
                                 start=(k == 0), stop=(k == HB - 1))
            last.then_inc(w2beta_filled, 1)
            pe.wait_ge(W2T_lo_ready, 2)

            def step(i, q, half, prepare, head, tail):
                nq = 1 - q
                if tail:
                    pe.wait_ge(y1_hi_ready, 2 * i)
                    pe.wait_ge(y1_lo_ready, 2 * i)
                    if not (isinstance(i, int) and i < 2):
                        pe.wait_ge(exp_ready, i - 1)
                        pe.wait_ge(p_ready, i - 1)
                    gather_edges(nq, halves_of(gy_hi), halves_of(gy_lo), (2, 3), m2_filled)
                if head:
                    pe.wait_ge(m1_lo_ready, 2 * i + 2)
                    pe.wait_ge(HT_ready, NB * i + NB)
                    if tail and not (isinstance(i, int) and i < 2):
                        pe.wait_ge(scored, NB * i - NB)
                    for d in range(DB):
                        for e in range(NB):
                            for part in (m1_hi, m1_lo):
                                last = pe.matmul(bank[4 + d][:, :], halves_of(part)[:, e, cols(d)], HT[q][:, e, :],
                                                 start=(e == 0 and part is m1_hi), stop=(e == NB - 1 and part is m1_lo))
                        last.then_inc(g_filled, 1)
                if tail:
                    pe.wait_ge(m2_lo_ready, 2 * i)
                    for c in range(NB):
                        for e in range(NB):
                            for part in (m2_hi, m2_lo):
                                last = pe.matmul(bank[6 + c // 2][:, cols(c % 2, D)], HT[nq][:, e, cols(c)],
                                                 halves_of(part)[:, e, :],
                                                 start=(e == 0 and part is m2_hi), stop=(e == NB - 1 and part is m2_lo))
                        if c % 2:
                            last.then_inc(y2_filled, 1)
                if head:
                    pe.wait_ge(g_hi_ready, 2 * i + 2)
                    pe.wait_ge(g_lo_ready, 2 * i + 2)
                    if isinstance(i, int) and i == 0:
                        pe.wait_ge(w2beta_ready, 1)
                        pe.wait_ge(M_lo_ready, 1)
                    for c in range(NB):
                        for d in range(DB):
                            for g, w in ((gy_hi, W1T_hi), (gy_hi, W1T_lo), (gy_lo, W1T_hi)):
                                last = pe.matmul(bank[c][:, :], g[:, d, cols(c)], w[:, d, :],
                                                 start=(d == 0 and g is gy_hi and w is W1T_hi),
                                                 stop=(d == DB - 1 and g is gy_lo))
                        last.then_inc(z_filled, 1)
                if prepare:
                    pe.wait_ge(H_bf_ready, NB * i + 2 * NB)
                    if tail:
                        pe.wait_ge(y2_ready, 2 * i)
                    else:
                        pe.wait_ge(WqkT_f_ready, 2)
                    transpose_H(0)
                if tail:
                    pe.wait_ge(x1_ready, i)
                    pe.wait_ge(x1_end_ready, i)
                    if not head:
                        pe.wait_ge(scored, NB * i - NB)
                    for d in range(DB):
                        for c in range(NB):
                            last = pe.transpose(bank[4 + d][:, cols(c)], x1[:, c, cols(d)], ident[:, :])
                        last.then_inc(x1T_filled, 1)
                if prepare:
                    transpose_H(1)
                if tail:
                    if head:
                        pe.wait_ge(z_ready, NB * i + NB)
                    for d in range(DB):
                        pe.wait_ge(x1T_hi_ready, 2 * i - 1 + d)
                        for a in range(DB):
                            for w in (M_hi, M_lo):
                                pe.matmul(bank[2 + a][:, :], w[:, d, cols(a)], x1T_hi[:, d, :],
                                          start=(d == 0 and w is M_hi), stop=False)
                    pe.wait_ge(x1T_lo_ready, 2 * i)
                    for a in range(DB):
                        for d in range(DB):
                            last = pe.matmul(bank[2 + a][:, :], M_hi[:, d, cols(a)], x1T_lo[:, d, :],
                                             start=False, stop=(d == DB - 1))
                        last.then_inc(xmT_filled, 1)
                    for c in range(NB):
                        for s, w in ((x1T_hi, Wv_hi), (x1T_hi, Wv_lo), (x1T_lo, Wv_hi)):
                            for d in range(DB):
                                last = pe.matmul(bank[4 + c // 2][:, cols(c % 2, D)], s[:, d, cols(c)], w[:, d, :],
                                                 start=(d == 0 and s is x1T_hi and w is Wv_hi),
                                                 stop=(d == DB - 1 and s is x1T_lo))
                        if c % 2:
                            last.then_inc(v_filled, 1)
                if head:
                    pe.wait_ge(n1_ready, i + 1)
                    pe.wait_ge(n1_end_ready, i + 1)
                    if prepare:
                        pe.wait_ge(HT_ready, NB * i + 2 * NB)
                    for k, to in enumerate((6, 7, 0, 1)):
                        for c in range(NB):
                            last = pe.transpose(bank[to][:, cols(c)], z[:, c, cols(k)], ident[:, :])
                        last.then_inc(n1T_filled, 1)
                if tail:
                    pe.wait_ge(xmT_hi_ready, 2 * i)
                    pe.wait_ge(xmT_lo_ready, 2 * i)
                    for c in range(NB):
                        if c >= 2:
                            pe.wait_ge(v_ready, 2 * i - 3 + c)
                        for s, r in ((xmT_hi, x1T_hi), (xmT_hi, x1T_lo), (xmT_lo, x1T_hi)):
                            for d in range(DB):
                                last = pe.matmul(bank[2 + c][:, :], s[:, d, cols(c)], r[:, d, :],
                                                 start=(d == 0 and s is xmT_hi and r is x1T_hi),
                                                 stop=(d == DB - 1 and s is xmT_lo))
                        last.then_inc(S_filled, 1)

                def make_y1(c, blocks=range(HB)):
                    for k in blocks:
                        for s, w in ((n1T_hi, W2T_hi), (n1T_hi, W2T_lo), (n1T_lo, W2T_hi)):
                            last = pe.matmul(bank[6 + c // 2][:, cols(c % 2, D)], s[:, k, cols(c)], w[:, k, :],
                                             start=(k == 0 and s is n1T_hi and w is W2T_hi),
                                             stop=(k == HB - 1 and s is n1T_lo))
                    if c % 2 and HB - 1 in blocks:
                        last.then_inc(y1_filled, 1)

                if head:
                    pe.wait_ge(n1T_hi_ready, HB * i + HB)
                    pe.wait_ge(n1T_lo_ready, HB * i + HB)
                    make_y1(0)
                if tail:
                    pe.wait_ge(w_ready, i)
                    for c in range(NB):
                        last = pe.transpose(bank[2][0:1, cols(c)], w_masked[:, c:c + 1], ident[:, :])
                    last.then_inc(w_filled, 1)
                if head:
                    make_y1(1)
                    make_y1(2)
                if tail:
                    pe.wait_ge(p_row_ready, i)
                if head:
                    make_y1(3, range(0, 1))
                if tail:
                    for c in range(NB):
                        last = pe.transpose(bank[3][:, c:c + 1], p_row[0:1, cols(c)], ident[0:1, 0:1])
                    last.then_inc(p_filled, 1)
                if head:
                    make_y1(3, range(1, HB))
                if prepare:
                    make_m1(i + 1, nq)

            def halves_of(part):
                return part.rearrange("p a (k d) -> p (a k) d", d=D)

            steps(pe, step)

        @block.scalar
        def _(act):
            def copy_HT(q, b, h):
                act.wait_ge(HT_filled, 2 * b + h + 1)
                for k in range(2):
                    act.activation(HT[q][:, 2 * h + k, :], HT_bank[h][:, cols(k, N)], ACT.Copy,
                                   accum_out=count[q][:, 2 * h + k:2 * h + k + 1]).then_inc(HT_ready, 1)

            def rounded(to, frm, filled, filled_at, ready):
                act.wait_ge(filled, filled_at)
                act.activation(to, frm, ACT.Copy).then_inc(ready, 1)

            def edges_hi(m_hi, q, filled, first_bank, b2, ready):
                for h in range(2):
                    act.wait_ge(filled, b2 + h + 1)
                    for k in range(2):
                        last = act.activation(m_hi[:, h, cols(k, D)], bank[first_bank + h][:, cols(k, D)], ACT.Identity,
                                              scale=Be[q][:, 2 * h + k:2 * h + k + 1], bias=0.0)
                    last.then_inc(ready, 1)

            def normalise(n, to, frm, blocks):
                for k in blocks:
                    last = act.activation(to[:, k, :], frm[:, k, :], ACT.Identity,
                                          scale=rstd[n][:, k:k + 1], bias=shift[n][:, k:k + 1])
                return last

            copy_HT(0, 0, 0)
            copy_HT(0, 0, 1)
            act.wait_ge(x_in[0], 16)
            act.activation(x_hi[:, :, :], x_raw[0][:, :, :], ACT.Copy).then_inc(x_hi_ready, 1)
            for d in range(DB):
                rounded(W1T_hi[:, d, :], bank[2 + d][:, :], W1T_filled, d + 1, W1T_hi_ready)
            act.wait_ge(columns_loaded, 32)
            for h in range(2):
                act.wait_ge(W2T_filled, h + 1)
                for k in range(2 * h, 2 * h + 2):
                    last = act.activation(W2T_hi[:, k, :], bank[4 + h][:, cols(k % 2, D)], ACT.Identity,
                                          scale=gamma_col[:, k:k + 1], bias=0.0)
                act.activation(W2T_f[:, 2 * h:2 * h + 2, :], halves(bank[4 + h][:, :]), ACT.Copy).then_inc(W2T_f_ready, 1)
            for h in range(2):
                rounded(WqkT_f[:, 2 * h:2 * h + 2, :], halves(bank[6 + h][:, :]), WqkT_filled, h + 1, WqkT_f_ready)
            act.wait_ge(Be_ready, 1)
            edges_hi(m1_hi, 0, m1_filled, 0, 0, m1_hi_ready)
            rounded(M_hi[:, :, :], halves(bank[3][:, :]), M_filled, 1, M_hi_ready)
            act.wait_ge(Wv_loaded, 16)
            act.activation(Wv_hi[:, :, :], Wv_in, ACT.Copy).then_inc(Wv_hi_ready, 1)
            act.wait_ge(w2beta_filled, 1)
            act.activation(w2beta[:, 0, :], bank[2][:, 0:D], ACT.Copy)
            act.activation(w2beta[:, 1, :], bank[2][:, 0:D], ACT.Copy).then_inc(w2beta_ready, 1)

            def step(i, q, half, prepare, head, tail):
                nq = 1 - q
                if tail:
                    edges_hi(m2_hi, nq, m2_filled, 2, 2 * i - 2, m2_hi_ready)
                if head:
                    for d in range(DB):
                        rounded(gy_hi[:, d, :], bank[4 + d][:, :], g_filled, 2 * i + d + 1, g_hi_ready)
                if prepare:
                    act.wait_ge(x_in[nq], 16 * (half + q) + 16)
                    act.wait_ge(m1_filled, 2 * i + 2)
                    act.activation(x_hi[:, :, :], x_raw[nq][:, :, :], ACT.Copy).then_inc(x_hi_ready, 1)

                def relu(c):
                    act.wait_ge(z_ready, NB * i + c + 1)
                    act.activation(z[:, c, :], z[:, c, :], ACT.Relu).then_inc(relu_ready, 1)

                if head:
                    relu(0)
                if tail:
                    act.wait_ge(shift_ready[1], i)
                    normalise(1, x1, y2, (0, 1)).then_inc(x1_ready, 1)
                if head:
                    relu(1)
                    relu(2)
                if tail:
                    for d in range(DB):
                        rounded(x1T_hi[:, d, :], bank[4 + d][:, :], x1T_filled, 2 * i - 1 + d, x1T_hi_ready)
                if head:
                    relu(3)
                if prepare:
                    copy_HT(nq, i + 1, 0)
                    copy_HT(nq, i + 1, 1)
                if tail:
                    for d in range(DB):
                        rounded(xmT_hi[:, d, :], bank[2 + d][:, :], xmT_filled, 2 * i - 1 + d, xmT_hi_ready)
                if head:
                    act.wait_ge(shift_ready[0], i + 1)
                    normalise(0, z, z, (0, 1)).then_inc(n1_ready, 1)
                if tail:
                    for h in range(2):
                        rounded(v[:, h, :], bank[4 + h][:, :], v_filled, 2 * i - 1 + h, v_ready)
                if head:
                    for k, frm in enumerate((6, 7, 0, 1)):
                        rounded(n1T_hi[:, k, :], bank[frm][:, :], n1T_filled, HB * i + k + 1, n1T_hi_ready)

                def y1_hi(h):
                    act.wait_ge(y1_ready, 2 * i + h + 1)
                    act.activation(gy_hi[:, h, :], y1[:, h, :], ACT.Copy).then_inc(y1_hi_ready, 1)

                if tail:
                    act.wait_ge(bias_ready, i)
                    act.activation(exps[0:1, :], bank[2][0:1, :], ACT.Exp, scale=SCALE, bias=w_bias[0:1, 0:1],
                                   accum_out=exp_sum[0:1, 0:1]).then_inc(exp_ready, 1)
                if head:
                    y1_hi(0)
                    y1_hi(1)
                if prepare:
                    act.wait_ge(Be_ready, i + 2)
                    edges_hi(m1_hi, nq, m1_filled, 0, 2 * i + 2, m1_hi_ready)
                if tail:
                    act.wait_ge(shift_ready[2], i)
                    if not (isinstance(i, int) and i < 2):
                        act.wait_ge(stored, 16 * i - 16)
                    normalise(2, result, y2, (0, 1)).then_inc(result_ready, 1)

            steps(act, step)

        @block.vector
        def _(dve):
            def lo_of(to, frm, hi, hi_ready, hi_at, ready):
                dve.wait_ge(hi_ready, hi_at)
                dve.tensor_tensor(to, frm, hi.bitcast(F32), ALU.subtract).then_inc(ready, 1)

            def edges_lo(m_lo, m_hi, q, first_bank, h, at, hi_ready, ready):
                dve.wait_ge(hi_ready, at)
                for k in range(2):
                    last = dve.scalar_tensor_tensor(m_lo[:, h, cols(k, D)], bank[first_bank + h][:, cols(k, D)],
                                                    Be[q][:, 2 * h + k:2 * h + k + 1],
                                                    m_hi[:, h, cols(k, D)].bitcast(F32), ALU.mult, ALU.subtract)
                last.then_inc(ready, 1)

            def make_H(q):
                dve.tensor_scalar(H[q][:, :, :], adj_raw[q][:, :, :], 0.0, None, ALU.not_equal).then_inc(H_ready, 1)

            def make_H_bf(q, blocks):
                for c in blocks:
                    dve.tensor_scalar(H_bf[:, c, :], adj_raw[q][:, c, :], 0.0, None, ALU.not_equal).then_inc(H_bf_ready, 1)

            def normalise_end(n, to, frm):
                for k in (2, 3):
                    last = dve.tensor_scalar(to[:, k, :], frm[:, k, :], rstd[n][:, k:k + 1], shift[n][:, k:k + 1],
                                             ALU.mult, ALU.add)
                return last

            def guarded_inverse(to, frm, floor, scratch, frm_ready, frm_at, mid_ready, mid_at, ready):
                dve.wait_ge(frm_ready, frm_at)
                dve.tensor_scalar(scratch, frm, floor, None, ALU.max).then_inc(mid_ready, 1)
                dve.wait_ge(mid_ready, mid_at + 1)
                dve.reciprocal(to, scratch).then_inc(mid_ready, 1)
                dve.wait_ge(mid_ready, mid_at + 2)
                dve.scalar_tensor_tensor(to, frm, 0.0, to, ALU.is_gt, ALU.mult).then_inc(ready, 1)

            def make_Be(b, q):
                guarded_inverse(Be[q][:, :], count[q][:, :], 0.5, inv_count[:, :], HT_ready, NB * b + NB,
                                count_inv_ready, 2 * b, Be_ready)

            def sum_degree(q, blocks):
                for c in blocks:
                    dve.scalar_tensor_tensor(unused[:, c, :], adj_raw[q][:, c, :], 0.0, row0[q][:, :], ALU.not_equal,
                                             ALU.mult, accum_out=degree[:, c:c + 1]).then_inc(degree_ready, 1)

            def make_Dn(b, q):
                guarded_inverse(Dn[q][:, :], degree[:, :], TINY, inv_degree[:, :], degree_ready, NB * b + NB,
                                degree_inv_ready, 2 * b, Dn_ready)

            def take_stats(n, frm, k):
                dve.bn_stats(stats[n][:, k, :], frm[:, k, :]).then_inc(stats_ready[n], 1)

            def await_stats(n, b):
                dve.wait_ge(stats_ready[n], 4 * b + 4)

            def take_moments(n):
                for k in range(4):
                    last = dve.bn_aggr(moments[n][:, k, :], stats[n][:, k, :])
                last.then_inc(moments_ready[n], 1)

            def take_shift(n, b):
                dve.wait_ge(rstd_ready[n], b + 1)
                dve.scalar_tensor_tensor(shift[n][:, :], moments[n][:, :, 0], -1.0, rstd[n][:, :],
                                         ALU.mult, ALU.mult).then_inc(shift_ready[n], 1)

            dve.memset(ones[:, :], 1.0).then_inc(ones_ready, 1)
            dve.wait_ge(adj_in[0], 16)
            make_H_bf(0, range(NB))
            make_H(0)
            dve.wait_ge(ident_ready, 1)
            dve.tensor_copy(ident_bf[:, :], ident[:, :]).then_inc(ident_bf_ready, 1)
            dve.wait_ge(row0_in[0], 16)
            sum_degree(0, range(NB))
            make_Dn(0, 0)
            dve.wait_ge(columns_loaded, 32)
            dve.wait_ge(ones_ready, 1)
            for k in range(HB):
                last = dve.tensor_scalar(beta_wide[:, k, :], ones[:, :], beta_col[:, k:k + 1], None, ALU.mult)
            last.then_inc(beta_ready, 1)
            for d in range(DB):
                lo_of(W1T_lo[:, d, :], bank[2 + d][:, :], W1T_hi[:, d, :], W1T_hi_ready, d + 1, W1T_lo_ready)
            make_Be(0, 0)
            for h in range(2):
                dve.wait_ge(W2T_f_ready, h + 1)
                for k in range(2 * h, 2 * h + 2):
                    last = dve.scalar_tensor_tensor(W2T_lo[:, k, :], bank[4 + h][:, cols(k % 2, D)],
                                                    gamma_col[:, k:k + 1], W2T_hi[:, k, :].bitcast(F32),
                                                    ALU.mult, ALU.subtract)
                last.then_inc(W2T_lo_ready, 1)
            dve.wait_ge(Be_ready, 1)
            for h in range(2):
                edges_lo(m1_lo, m1_hi, 0, 0, h, h + 1, m1_hi_ready, m1_lo_ready)
            lo_of(M_lo[:, :, :], halves(bank[3][:, :]), M_hi[:, :, :], M_hi_ready, 1, M_lo_ready)
            lo_of(Wv_lo[:, :, :], Wv_in, Wv_hi[:, :, :], Wv_hi_ready, 1, Wv_lo_ready)
            dve.wait_ge(rows_loaded, 48)
            dve.wait_ge(w2beta_ready, 1)

            def step(i, q, half, prepare, head, tail):
                nq = 1 - q
                if tail:
                    edges_lo(m2_lo, m2_hi, nq, 2, 0, 2 * i - 1, m2_hi_ready, m2_lo_ready)
                    edges_lo(m2_lo, m2_hi, nq, 2, 1, 2 * i, m2_hi_ready, m2_lo_ready)
                if prepare:
                    dve.wait_ge(adj_in[nq], 16 * (half + q) + 16)
                    make_H_bf(nq, (0, 1))
                if head:
                    for d in range(DB):
                        lo_of(gy_lo[:, d, :], bank[4 + d][:, :], gy_hi[:, d, :], g_hi_ready, 2 * i + d + 1, g_lo_ready)
                if prepare:
                    make_H_bf(nq, (2,))
                if tail:
                    dve.wait_ge(base_ready, i)
                    if not (isinstance(i, int) and i < 2):
                        dve.wait_ge(result_ready, i - 1)
                    for h in range(2):
                        dve.wait_ge(y2_filled, 2 * i - 1 + h)
                        for c in range(2 * h, 2 * h + 2):
                            last = dve.scalar_tensor_tensor(y2[:, c, :], bank[6 + h][:, cols(c % 2, D)],
                                                            Dn[nq][:, c:c + 1], base[:, c, :], ALU.mult, ALU.add)
                        last.then_inc(y2_ready, 1)
                        dve.wait_ge(y2_ready, 2 * i - 1 + h)
                        for c in range(2 * h, 2 * h + 2):
                            take_stats(1, y2, c)
                    await_stats(1, i - 1)
                if prepare:
                    make_H_bf(nq, (3,))
                if tail:
                    take_moments(1)

                def make_z(c):
                    dve.wait_ge(z_filled, NB * i + c + 1)
                    dve.scalar_tensor_tensor(z[:, c, :], bank[c][:, :], Dn[q][:, c:c + 1], b1_row[:, :],
                                             ALU.mult, ALU.add).then_inc(z_ready, 1)

                def relu_stats(c):
                    dve.wait_ge(relu_ready, NB * i + c + 1)
                    take_stats(0, z, c)

                if head:
                    dve.wait_ge(Dn_ready, i + 1)
                    make_z(0)
                if head:
                    make_z(1)
                if tail:
                    take_shift(1, i - 1)
                    dve.wait_ge(shift_ready[1], i)
                    normalise_end(1, x1, y2).then_inc(x1_end_ready, 1)
                if head:
                    relu_stats(0)
                    make_z(2)
                    relu_stats(1)
                    make_z(3)
                    relu_stats(2)
                    relu_stats(3)
                    await_stats(0, i)
                if prepare:
                    dve.wait_ge(row0_in[nq], 16 * (half + q) + 16)
                    sum_degree(nq, range(0, 1))
                if head:
                    take_moments(0)
                if tail:
                    lo_of(x1T_lo[:, 0, :], bank[4][:, :], x1T_hi[:, 0, :], x1T_hi_ready, 2 * i - 1, x1T_lo_ready)
                    lo_of(x1T_lo[:, 1, :], bank[5][:, :], x1T_hi[:, 1, :], x1T_hi_ready, 2 * i, x1T_lo_ready)
                if head:
                    take_shift(0, i)
                    dve.wait_ge(shift_ready[0], i + 1)
                    normalise_end(0, z, z).then_inc(n1_end_ready, 1)
                if prepare:
                    make_H(nq)
                if tail:
                    lo_of(xmT_lo[:, 0, :], bank[2][:, :], xmT_hi[:, 0, :], xmT_hi_ready, 2 * i - 1, xmT_lo_ready)
                    lo_of(xmT_lo[:, 1, :], bank[3][:, :], xmT_hi[:, 1, :], xmT_hi_ready, 2 * i, xmT_lo_ready)
                if prepare:
                    sum_degree(nq, range(1, NB))
                    make_Dn(i + 1, nq)
                    make_Be(i + 1, nq)
                if head:
                    for k, frm in enumerate((6, 7, 0, 1)):
                        lo_of(n1T_lo[:, k, :], bank[frm][:, :], n1T_hi[:, k, :], n1T_hi_ready, HB * i + k + 1, n1T_lo_ready)
                if tail:
                    dve.wait_ge(masked_ready, NB * i)
                    for c in range(NB):
                        dve.wait_ge(S_filled, NB * i - NB + c + 1)
                        dve.tensor_tensor_reduce(out=unused[:, c, :], in0=bank[2 + c][:, :], in1=adj_masked[nq][:, c, :],
                                                 scale=1.0, scalar=0.0, op0=ALU.mult, op1=ALU.add,
                                                 accum_out=w_sum[:, c:c + 1]).then_inc(scored, 1)
                    dve.wait_ge(scored, NB * i)
                    dve.tensor_tensor(w_masked[:, :], w_sum[:, :], mask_col[:, i - 1, :], ALU.mult).then_inc(w_ready, 1)

                def make_y1(h):
                    dve.wait_ge(y1_filled, 2 * i + h + 1)
                    dve.tensor_tensor(y1[:, h, :], bank[6 + h][:, :], w2beta[:, :, :].rearrange("p a d -> p (a d)"),
                                      ALU.add).then_inc(y1_ready, 1)

                if tail:
                    dve.wait_ge(w_filled, i)
                    dve.tensor_reduce(w_max[:, :], bank[2][0:1, :], AX_X, ALU.max).then_inc(max_ready, 1)
                    dve.wait_ge(max_ready, i)
                    dve.tensor_scalar(w_bias[:, :], w_max[:, :], -SCALE, None, ALU.mult).then_inc(bias_ready, 1)
                if head:
                    make_y1(0)
                if tail:
                    dve.wait_ge(exp_ready, i)
                    dve.reciprocal(exp_inv[:, :], exp_sum[:, :]).then_inc(exp_inv_ready, 1)
                    dve.wait_ge(exp_inv_ready, i)
                    dve.tensor_scalar(p_row[:, :], exps[:, :], exp_inv[:, :], None, ALU.mult).then_inc(p_row_ready, 1)

                def make_y3(c):
                    dve.scalar_tensor_tensor(y2[:, c, :], v[:, c // 2, cols(c % 2, D)], p_col[:, c:c + 1],
                                             x1[:, c, :], ALU.mult, ALU.add).then_inc(y3_ready, 1)

                if tail:
                    dve.wait_ge(p_filled, i)
                    dve.tensor_copy(p_col[:, :], bank[3][:, 0:NB]).then_inc(p_ready, 1)
                    dve.wait_ge(p_ready, i)
                    make_y3(0)
                    make_y3(1)
                if head:
                    make_y1(1)
                if tail:
                    make_y3(2)
                    make_y3(3)
                    for c in range(NB):
                        dve.wait_ge(y3_ready, NB * i - NB + c + 1)
                        take_stats(2, y2, c)
                    await_stats(2, i - 1)
                if prepare:
                    edges_lo(m1_lo, m1_hi, nq, 0, 0, 2 * i + 3, m1_hi_ready, m1_lo_ready)
                if tail:
                    take_moments(2)
                if prepare:
                    edges_lo(m1_lo, m1_hi, nq, 0, 1, 2 * i + 4, m1_hi_ready, m1_lo_ready)
                if tail:
                    take_shift(2, i - 1)
                    dve.wait_ge(shift_ready[2], i)
                    if not (isinstance(i, int) and i < 2):
                        dve.wait_ge(stored, 16 * i - 16)
                    normalise_end(2, result, y2).then_inc(result_end_ready, 1)

            steps(dve, step)

        @block.gpsimd
        def _(pool):
            def x_low(b, q):
                pool.wait_ge(x_hi_ready, b + 1)
                pool.tensor_tensor(x_lo[:, :, :], x_raw[q][:, :, :], x_hi[:, :, :].bitcast(F32),
                                   ALU.subtract).then_inc(x_lo_ready, 1)

            def inverse_std(n, b):
                pool.wait_ge(moments_ready[n], b + 1)
                pool.tensor_tensor(varp[n][:, :], moments[n][:, :, 1], eps_col[:, :], ALU.add)\
                    .then_inc(varp_ready[n], 1)
                pool.wait_ge(varp_ready[n], b + 1)
                pool.tensor_tensor(rstd[n][:, :], varp[n][:, :], minus_half[:, :], ALU.pow).then_inc(rstd_ready[n], 1)

            pool.memset(minus_half[:, :], -0.5).then_inc(half_ready, 1)
            pool.memset(eps_col[:, :], EPS).then_inc(half_ready, 1)
            pool.memset(ident[:, :], 0.0).then_inc(ident_zero, 1)
            pool.wait_ge(ident_zero, 1)
            pool.affine_select(out=ident[:, :], in_=ident[:, :], compare_op=ALU.not_equal, fill=1.0, base=0,
                               pattern=[[-1, P]], channel_multiplier=1).then_inc(ident_ready, 1)
            x_low(0, 0)
            pool.wait_ge(half_ready, 2)
            pool.wait_ge(rows_loaded, 48)
            pool.wait_ge(W1T_filled, DB)
            pool.wait_ge(W2T_filled, 2)
            pool.wait_ge(WqkT_filled, 2)
            pool.wait_ge(Wv_lo_ready, 1)

            def step(i, q, half, prepare, head, tail):
                nq = 1 - q
                if head:
                    pool.wait_ge(maskrow_in[q], 16 * half + 16)
                    pool.wait_ge(adj_in[q], 16 * half + 16)
                    if not (isinstance(i, int) and i < 2):
                        pool.wait_ge(scored, NB * i - NB)
                    for c in range(NB):
                        pool.tensor_tensor(adj_masked[q][:, c, :].rearrange("p (k n) -> p k n", k=NB),
                                           adj_raw[q][:, c, :].rearrange("p (n k) -> p k n", k=NB),
                                           maskrow[q][:, :].rearrange("p (n k) -> p k n", k=NB),
                                           ALU.mult).then_inc(masked_ready, 1)
                if prepare:
                    x_low(i + 1, nq)
                if tail:
                    inverse_std(1, i - 1)
                if head:
                    if tail:
                        pool.wait_ge(y2_ready, 2 * i)
                    pool.tensor_tensor(base[:, :, :], x_raw[q][:, :, :], x_raw[q][:, :, :], ALU.add)\
                        .then_inc(twice_ready, 1)
                    pool.wait_ge(twice_ready, i + 1)
                    pool.tensor_tensor(base[:, :, :], base[:, :, :],
                                       b2_row[:, :].rearrange("p (a d) -> p a d", a=1).to_broadcast([P, NB, D]),
                                       ALU.add).then_inc(base_ready, 1)
                    inverse_std(0, i)

                def y1_low(h):
                    pool.wait_ge(y1_hi_ready, 2 * i + h + 1)
                    pool.tensor_tensor(gy_lo[:, h, :], y1[:, h, :], gy_hi[:, h, :].bitcast(F32),
                                       ALU.subtract).then_inc(y1_lo_ready, 1)

                if head:
                    y1_low(0)
                    y1_low(1)
                if tail:
                    inverse_std(2, i - 1)

            steps(pool, step)


_INS = ['x', 'adj', 'nodemask', 'L0_gnn_W1', 'L0_gnn_b1', 'L0_gnn_gamma', 'L0_gnn_beta', 'L0_gnn_W2', 'L0_gnn_b2',
        'L1_gnn_Wqk', 'L1_gnn_Wv']


def kernel(**inputs):
    import numpy as _np
    import concourse.bacc as _bacc
    from concourse import mybir as _mybir
    from concourse.bass_utils import run_bass_kernel_spmd as _run

    nc = _bacc.Bacc("TRN2", target_bir_lowering=False, num_devices=1)
    arrays, args = {}, []
    for name in _INS:
        a = _np.ascontiguousarray(inputs[name])
        arrays[f"in_{name}_dram"] = a
        args.append(nc.dram_tensor(f"in_{name}_dram", a.shape, _mybir.dt.from_np(a.dtype), kind="ExternalInput").ap())
    shape = inputs['x'].shape
    args.append(nc.dram_tensor("out_dram", shape, _mybir.dt.from_np(_np.dtype('float32')), kind="ExternalOutput").ap())
    graph_kernel(nc, *args)
    r = _run(nc, [arrays], core_ids=[0])
    return r.results[0]["out_dram"]
```

```python
from contextlib import ExitStack

import concourse.bass as bass
from concourse import mybir

P = 128
F32 = mybir.dt.float32
F32R = mybir.dt.float32r
BF16 = mybir.dt.bfloat16
ALU = mybir.AluOpType
ACT = mybir.ActivationFunctionType
AX_X = mybir.AxisListType.X
EPS = 1e-5
TINY = 1.17549435e-38



def graph_kernel(nc, x, adj, nodemask, W1, b1, gamma, beta, W2, b2, Wqk, Wv, out):
    B, N, D = x.shape
    HID = W1.shape[0]
    NB = N // P
    DB = D // P
    HB = HID // P
    BANK = 512
    assert NB == 4 and DB == 2 and HB == 4 and N == BANK and HID == BANK and Wqk.shape[1] == 2 * D
    SCALE = float(D) ** -0.5
    WARMING = 18

    with ExitStack() as ctx:
        def sb(name, shape, dt=F32):
            return ctx.enter_context(nc.sbuf_tensor(name, shape, dt))

        def sem(name):
            return ctx.enter_context(nc.semaphore(name))

        bank = [ctx.enter_context(nc.psum_tensor(f"bank{i}", [P, BANK], F32)) for i in range(8)]

        def HT_banks(b):
            first = 4 if isinstance(b, int) and b == 1 else 6
            return [bank[first + h][:, :].bitcast(BF16) for h in range(2)]

        S_bank = (0, 1, 4, 5)
        n1T_bank = (6, 7, 2, 3)

        adj_raw = [sb(f"adj_raw{q}", [P, NB, N]) for q in range(2)]
        adj_masked = [sb(f"adj_masked{q}", [P, NB, N]) for q in range(2)]
        x_raw = [sb(f"x_raw{q}", [P, NB, D]) for q in range(2)]
        H = [sb(f"H{q}", [P, NB, N], F32R) for q in range(2)]
        H_bf = sb("H_bf", [P, NB, N], BF16)
        HT = [sb(f"HT{q}", [P, NB, N], F32R) for q in range(2)]
        row0 = [sb(f"row0_{q}", [P, N]) for q in range(2)]
        maskrow = [sb(f"maskrow{q}", [P, N]) for q in range(2)]
        count = [sb(f"count{q}", [P, NB]) for q in range(2)]
        Be = [sb(f"Be{q}", [P, NB]) for q in range(2)]
        Dn = [sb(f"Dn{q}", [P, NB]) for q in range(2)]
        x_hi = sb("x_hi", [P, NB, D], F32R)
        x_lo = sb("x_lo", [P, NB, D], F32R)
        base = sb("base", [P, NB, D])
        wide = sb("wide", [P, 2, NB, N], F32R)
        m1_hi, m1_lo = wide[:, 0, 0:2, :], wide[:, 0, 2:4, :]
        m2_hi, m2_lo = wide[:, 1, 0:2, :], wide[:, 1, 2:4, :]
        n1T_hi, n1T_lo = wide[:, 0], wide[:, 1]
        gy = sb("gy", [P, 2, 2, BANK], F32R)
        gy_hi, gy_lo = gy[:, 0], gy[:, 1]
        z = sb("z", [P, NB, HID])
        y1 = sb("y1", [P, 2, BANK])
        y2 = sb("y2", [P, NB, D])
        x1 = sb("x1", [P, NB, D])
        x1T_hi = sb("x1T_hi", [P, DB, N], F32R)
        x1T_lo = sb("x1T_lo", [P, DB, N], F32R)
        xmT_hi = sb("xmT_hi", [P, DB, N], F32R)
        xmT_lo = sb("xmT_lo", [P, DB, N], F32R)
        v = sb("v", [P, 2, BANK])
        result = sb("result", [P, NB, D])
        unused = sb("unused", [P, NB, N])
        exps, p_row = sb("exps", [1, N]), sb("p_row", [1, N])
        degree = sb("degree", [P, NB])
        inv_count, inv_degree = sb("inv_count", [P, NB]), sb("inv_degree", [P, NB])
        stats = [sb(f"stats{n}", [P, 4, 6]) for n in range(3)]
        moments = [sb(f"moments{n}", [P, 4, 2]) for n in range(3)]
        varp = [sb(f"varp{n}", [P, 4]) for n in range(3)]
        rstd = [sb(f"rstd{n}", [P, 4]) for n in range(3)]
        shift = [sb(f"shift{n}", [P, 4]) for n in range(3)]
        minus_half, eps_col = sb("minus_half", [P, 4]), sb("eps_col", [P, 4])
        w_sum, w_masked, p_col = sb("w_sum", [P, NB]), sb("w_masked", [P, NB]), sb("p_col", [P, NB])
        w_max, w_bias = sb("w_max", [1, 1]), sb("w_bias", [1, 1])
        exp_sum, exp_inv = sb("exp_sum", [1, 1]), sb("exp_inv", [1, 1])
        ident, ident_bf, ones = sb("ident", [P, P]), sb("ident_bf", [P, P], BF16), sb("ones", [P, P])
        mask_col = sb("mask_col", [P, B, NB])
        b1_row, b2_row = sb("b1_row", [P, HID]), sb("b2_row", [P, D])
        gamma_col, beta_col = sb("gamma_col", [P, HB]), sb("beta_col", [P, HB])
        W1T_hi, W1T_lo = sb("W1T_hi", [P, DB, HID], F32R), sb("W1T_lo", [P, DB, HID], F32R)
        W2T_hi, W2T_lo = sb("W2T_hi", [P, HB, D], F32R), sb("W2T_lo", [P, HB, D], F32R)
        M_hi, M_lo = sb("M_hi", [P, DB, D], F32R), sb("M_lo", [P, DB, D], F32R)
        Wv_hi, Wv_lo = sb("Wv_hi", [P, DB, D], F32R), sb("Wv_lo", [P, DB, D], F32R)
        w2beta = sb("w2beta", [P, 2, D])
        W1_in = z[:, 0:2, :].rearrange("p a n -> p (a n)").rearrange("p (k d) -> p k d", d=D)
        Wqk_in = z[:, 2:4, :]
        W2_in = v[:, :, :]
        Wv_in = result[:, 0:2, :]
        W2T_f = x1[:, :, :].rearrange("p a n -> p (a n)").rearrange("p (k d) -> p k d", d=D)
        WqkT_f = y2[:, :, :].rearrange("p a n -> p (a n)").rearrange("p (k d) -> p k d", d=D)
        beta_wide = y1[:, :, :].rearrange("p a n -> p (a n)")[:, 0:HB * P].rearrange("p (k n) -> p k n", n=P)

        adj_in = [sem(f"adj_in{q}") for q in range(2)]
        first_adj_in = [sem(f"first_adj_in{c}") for c in range(NB)]
        x_in = [sem(f"x_in{q}") for q in range(2)]
        row0_in = [sem(f"row0_in{q}") for q in range(2)]
        maskrow_in = [sem(f"maskrow_in{q}") for q in range(2)]
        W1_loaded, W2_loaded, Wqk_loaded = sem("W1_loaded"), sem("W2_loaded"), sem("Wqk_loaded")
        Wv_loaded, columns_loaded, rows_loaded = sem("Wv_loaded"), sem("columns_loaded"), sem("rows_loaded")
        stored = sem("stored")
        HT_filled, m1_filled, m2_filled, g_filled = sem("HT_filled"), sem("m1_filled"), sem("m2_filled"), sem("g_filled")
        y2_filled, z_filled, x1T_filled = sem("y2_filled"), sem("z_filled"), sem("x1T_filled")
        xmT_filled, v_filled, n1T_filled = sem("xmT_filled"), sem("v_filled"), sem("n1T_filled")
        S_filled, y1_filled, w_filled, p_filled = sem("S_filled"), sem("y1_filled"), sem("w_filled"), sem("p_filled")
        x_hi_ready, m1_hi_ready, m2_hi_ready, g_hi_ready = sem("x_hi_ready"), sem("m1_hi_ready"), sem("m2_hi_ready"), sem("g_hi_ready")
        relu_ready, x1_ready, HT_ready = sem("relu_ready"), sem("x1_ready"), sem("HT_ready")
        x1T_hi_ready, xmT_hi_ready, v_ready = sem("x1T_hi_ready"), sem("xmT_hi_ready"), sem("v_ready")
        n1_ready, n1T_hi_ready, exp_ready = sem("n1_ready"), sem("n1T_hi_ready"), sem("exp_ready")
        y1_hi_ready, result_ready = sem("y1_hi_ready"), sem("result_ready")
        first_H_ready = sem("first_H_ready")
        H_ready, H_bf_ready, Be_ready, Dn_ready = sem("H_ready"), sem("H_bf_ready"), sem("Be_ready"), sem("Dn_ready")
        m1_lo_ready, m2_lo_ready, g_lo_ready = sem("m1_lo_ready"), sem("m2_lo_ready"), sem("g_lo_ready")
        y2_ready, z_ready, x1T_lo_ready = sem("y2_ready"), sem("z_ready"), sem("x1T_lo_ready")
        xmT_lo_ready, n1T_lo_ready, scored = sem("xmT_lo_ready"), sem("n1T_lo_ready"), sem("scored")
        w_ready, y1_ready, bias_ready = sem("w_ready"), sem("y1_ready"), sem("bias_ready")
        exp_inv_ready, p_row_ready, p_ready, y3_ready = sem("exp_inv_ready"), sem("p_row_ready"), sem("p_ready"), sem("y3_ready")
        x1_end_ready, n1_end_ready, result_end_ready = sem("x1_end_ready"), sem("n1_end_ready"), sem("result_end_ready")
        max_ready, degree_ready = sem("max_ready"), sem("degree_ready")
        count_inv_ready, degree_inv_ready = sem("count_inv_ready"), sem("degree_inv_ready")
        stats_ready = [sem(f"stats_ready{n}") for n in range(3)]
        moments_ready = [sem(f"moments_ready{n}") for n in range(3)]
        shift_ready = [sem(f"shift_ready{n}") for n in range(3)]
        x_lo_ready, y1_lo_ready, masked_ready = sem("x_lo_ready"), sem("y1_lo_ready"), sem("masked_ready")
        base_ready, twice_ready = sem("base_ready"), sem("twice_ready")
        varp_ready = [sem(f"varp_ready{n}") for n in range(3)]
        rstd_ready = [sem(f"rstd_ready{n}") for n in range(3)]
        ident_zero, ident_ready, ident_bf_ready, half_ready, ones_ready = sem("ident_zero"), sem("ident_ready"), sem("ident_bf_ready"), sem("half_ready"), sem("ones_ready")
        beta_ready, W1T_filled, W2T_filled = sem("beta_ready"), sem("W1T_filled"), sem("W2T_filled")
        WqkT_filled, w2beta_filled, M_filled = sem("WqkT_filled"), sem("w2beta_filled"), sem("M_filled")
        W1T_hi_ready, W2T_hi_ready, W2T_f_ready, WqkT_f_ready = sem("W1T_hi_ready"), sem("W2T_hi_ready"), sem("W2T_f_ready"), sem("WqkT_f_ready")
        M_hi_ready, Wv_hi_ready, w2beta_ready = sem("M_hi_ready"), sem("Wv_hi_ready"), sem("w2beta_ready")
        W1T_lo_ready, W2T_lo_ready, M_lo_ready, Wv_lo_ready = sem("W1T_lo_ready"), sem("W2T_lo_ready"), sem("M_lo_ready"), sem("Wv_lo_ready")

        block = ctx.enter_context(nc.Block())

        def cols(k, n=P):
            return slice(k * n, (k + 1) * n)

        def adj_count(half, q):
            return 16 * half if q == 0 else 16 * half + 16

        def halves(bank_ap):
            return bank_ap.rearrange("p (k d) -> p k d", d=D)

        def steps(engine, step):
            step(0, 0, 0, True, True, False)
            step(1, 1, 0, True, True, True)
            with engine.Fori(1, B // 2 - 1) as t:
                step(2 * t, 0, t, True, True, True)
                step(2 * t + 1, 1, t, True, True, True)
            step(B - 2, 0, B // 2 - 1, True, True, True)
            step(B - 1, 1, B // 2 - 1, False, True, True)
            step(B, 0, B // 2, False, False, True)

        x_dram = x.rearrange("b (p k) d -> b p k d", k=NB)
        adj_dram = adj.rearrange("b (p k) e -> b p k e", k=NB)
        adj_rows, mask_rows = adj, nodemask.rearrange("b (a n) -> b a n", a=1)
        out_dram = out.rearrange("b (p k) d -> b p k d", k=NB)

        @block.sync
        def _(sp):
            def load(b, q):
                sp.dma_start(adj_raw[q][:, :, :], adj_dram[b]).then_inc(adj_in[q], 16)
                sp.dma_start(x_raw[q][:, :, :], x_dram[b]).then_inc(x_in[q], 16)
                sp.dma_start(row0[q][:, :], adj_rows[b, 0:1, :].to_broadcast([P, N])).then_inc(row0_in[q], 16)
                sp.dma_start(maskrow[q][:, :], mask_rows[b].to_broadcast([P, N])).then_inc(maskrow_in[q], 16)

            sp.dma_start(x_raw[0][:, :, :], x_dram[0]).then_inc(x_in[0], 16)
            for c in range(NB):
                sp.dma_start(adj_raw[0][:, c, :], adj_dram[0][:, c, :]).then_inc(first_adj_in[c], 16)
            sp.dma_start(row0[0][:, :], adj_rows[0, 0:1, :].to_broadcast([P, N])).then_inc(row0_in[0], 16)
            sp.dma_start(maskrow[0][:, :], mask_rows[0].to_broadcast([P, N])).then_inc(maskrow_in[0], 16)
            sp.dma_start(W1_in, W1.rearrange("(k p) d -> p k d", p=P)).then_inc(W1_loaded, 16)
            sp.dma_start(Wqk_in, Wqk.rearrange("(k p) a -> p k a", p=P)).then_inc(Wqk_loaded, 16)
            sp.dma_start(W2_in, W2.rearrange("(k p) h -> p k h", p=P)).then_inc(W2_loaded, 16)
            with nc.allow_non_contiguous_dma(reason="two columns of 512 numbers, once"):
                sp.dma_start(gamma_col[:, :], gamma.rearrange("(k p) -> p k", p=P)).then_inc(columns_loaded, 16)
                sp.dma_start(beta_col[:, :], beta.rearrange("(k p) -> p k", p=P)).then_inc(columns_loaded, 16)
            sp.dma_start(b1_row[:, :], b1.rearrange("(a h) -> a h", a=1).to_broadcast([P, HID])).then_inc(rows_loaded, 16)
            sp.dma_start(b2_row[:, :], b2.rearrange("(a d) -> a d", a=1).to_broadcast([P, D])).then_inc(rows_loaded, 16)
            sp.dma_start(mask_col[:, :, :], nodemask.rearrange("b (p k) -> p b k", k=NB)).then_inc(rows_loaded, 16)
            load(1, 1)
            sp.dma_start(Wv_in, Wv.rearrange("(k p) d -> p k d", p=P)).then_inc(Wv_loaded, 16)

            def step(i, q, half, prepare, head, tail):
                if prepare and not (isinstance(i, int) and i + 2 >= B):
                    if isinstance(i, int) and i == 0:
                        sp.wait_ge(first_H_ready, NB)
                    sp.wait_ge(x_hi_ready, i + 1)
                    sp.wait_ge(H_bf_ready, NB * i + NB)
                    sp.wait_ge(degree_ready, NB * i + NB)
                    sp.wait_ge(masked_ready, NB * i + NB)
                    sp.wait_ge(x_lo_ready, i + 1)
                    sp.wait_ge(base_ready, i + 1)
                    load(i + 2, q)
                if tail:
                    sp.wait_ge(result_ready, i)
                    sp.wait_ge(result_end_ready, i)
                    sp.dma_start(out_dram[i - 1], result[:, :, :]).then_inc(stored, 16)

            steps(sp, step)
            sp.wait_ge(stored, 16 * B)

        @block.tensor
        def _(pe):
            def transpose_H(b, h):
                for k in range(2):
                    for c in range(NB):
                        last = pe.transpose(HT_banks(b)[h][:, cols(NB * k + c)], H_bf[:, c, cols(2 * h + k)], ident_bf[:, :])
                last.then_inc(HT_filled, 1)

            def gather_edges(q, hi, lo, banks, filled):
                for k in range(NB):
                    for c in range(NB):
                        for part in (hi, lo):
                            last = pe.matmul(bank[banks[k // 2]][:, cols(k % 2, D)], H[q][:, c, cols(k)], part[:, c, :],
                                             start=(c == 0 and part is hi), stop=(c == NB - 1 and part is lo))
                    if k % 2:
                        last.then_inc(filled, 1)

            def make_m1(n, q):
                if isinstance(n, int) and n == 0:
                    pe.wait_ge(first_H_ready, NB)
                else:
                    pe.wait_ge(H_ready, n)
                pe.wait_ge(x_hi_ready, n + 1)
                pe.wait_ge(x_lo_ready, n + 1)
                gather_edges(q, x_hi, x_lo, (0, 1), m1_filled)

            pe.wait_ge(ident_ready, 1)
            for k in range(WARMING):
                pe.transpose(bank[0][:, cols(k % 4)], ident[:, :], ident[:, :])
            pe.wait_ge(ident_bf_ready, 1)
            for c in range(NB):
                pe.wait_ge(H_bf_ready, c + 1)
                for e in range(NB):
                    last = pe.transpose(HT_banks(0)[e // 2][:, cols(NB * (e % 2) + c)], H_bf[:, c, cols(e)], ident_bf[:, :])
                    if c == NB - 1 and e % 2:
                        last.then_inc(HT_filled, 1)
            make_m1(0, 0)
            pe.wait_ge(W1_loaded, 16)
            for d in range(DB):
                for k in range(HB):
                    last = pe.transpose(bank[2 + d][:, cols(k)], W1_in[:, k, cols(d)], ident[:, :])
                last.then_inc(W1T_filled, 1)
            pe.wait_ge(HT_ready, NB)
            pe.wait_ge(Wqk_loaded, 16)
            for k in range(4):
                for d in range(DB):
                    last = pe.transpose(bank[6 + k // 2][:, (k % 2) * D + d * P:(k % 2) * D + (d + 1) * P],
                                        Wqk_in[:, d, cols(k)], ident[:, :])
                if k % 2:
                    last.then_inc(WqkT_filled, 1)

            def transpose_W2():
                pe.wait_ge(W2_loaded, 16)
                pe.wait_ge(W1T_lo_ready, 2)
                for k in range(HB):
                    for d in range(DB):
                        last = pe.transpose(bank[2 + k // 2][:, (k % 2) * D + d * P:(k % 2) * D + (d + 1) * P],
                                            W2_in[:, d, cols(k)], ident[:, :])
                    if k % 2:
                        last.then_inc(W2T_filled, 1)

            def set_up_products():
                pe.wait_ge(WqkT_f_ready, 2)
                pe.wait_ge(z_ready, 2)
                for d in range(DB):
                    for a in range(2):
                        last = pe.matmul(bank[0][:, cols(d, D)], WqkT_f[:, a, cols(d)], WqkT_f[:, 2 + a, :],
                                         start=(a == 0), stop=(a == 1))
                last.then_inc(M_filled, 1)
                pe.wait_ge(W2T_f_ready, 2)
                pe.wait_ge(beta_ready, 1)
                for k in range(HB):
                    last = pe.matmul(bank[1][:, 0:D], beta_wide[:, k, :], W2T_f[:, k, :],
                                     start=(k == 0), stop=(k == HB - 1))
                last.then_inc(w2beta_filled, 1)

            def step(i, q, half, prepare, head, tail):
                nq = 1 - q
                if tail:
                    pe.wait_ge(y1_hi_ready, 2 * i)
                    pe.wait_ge(y1_lo_ready, 2 * i)
                    if not (isinstance(i, int) and i < 2):
                        pe.wait_ge(exp_ready, i - 1)
                        pe.wait_ge(p_ready, i - 1)
                    gather_edges(nq, halves_of(gy_hi), halves_of(gy_lo), (2, 3), m2_filled)
                if head:
                    pe.wait_ge(m1_lo_ready, 2 * i + 2)
                    pe.wait_ge(HT_ready, NB * i + NB)
                    if tail and not (isinstance(i, int) and i < 2):
                        pe.wait_ge(scored, NB * i - NB)
                    for d in range(DB):
                        for e in range(NB):
                            for part in (m1_hi, m1_lo):
                                last = pe.matmul(bank[4 + d][:, :], halves_of(part)[:, e, cols(d)], HT[q][:, e, :],
                                                 start=(e == 0 and part is m1_hi), stop=(e == NB - 1 and part is m1_lo))
                        last.then_inc(g_filled, 1)
                if isinstance(i, int) and i == 0:
                    transpose_W2()
                if tail:
                    pe.wait_ge(m2_lo_ready, 2 * i)
                    for c in range(NB):
                        for e in range(NB):
                            for part in (m2_hi, m2_lo):
                                last = pe.matmul(bank[6 + c // 2][:, cols(c % 2, D)], HT[nq][:, e, cols(c)],
                                                 halves_of(part)[:, e, :],
                                                 start=(e == 0 and part is m2_hi), stop=(e == NB - 1 and part is m2_lo))
                        if c % 2:
                            last.then_inc(y2_filled, 1)
                if head:
                    pe.wait_ge(g_hi_ready, 2 * i + 2)
                    pe.wait_ge(g_lo_ready, 2 * i + 2)
                    for c in range(NB):
                        if isinstance(i, int) and i == 0 and c >= 2:
                            pe.wait_ge(W2T_lo_ready, c - 1)
                        for d in range(DB):
                            for g, w in ((gy_hi, W1T_hi), (gy_hi, W1T_lo), (gy_lo, W1T_hi)):
                                last = pe.matmul(bank[c][:, :], g[:, d, cols(c)], w[:, d, :],
                                                 start=(d == 0 and g is gy_hi and w is W1T_hi),
                                                 stop=(d == DB - 1 and g is gy_lo))
                        last.then_inc(z_filled, 1)
                if isinstance(i, int) and i == 0:
                    set_up_products()
                if prepare:
                    pe.wait_ge(H_bf_ready, NB * i + 2 * NB)
                    if tail:
                        pe.wait_ge(y2_ready, 2 * i)
                    transpose_H(i + 1, 0)
                if tail:
                    pe.wait_ge(x1_ready, i)
                    pe.wait_ge(x1_end_ready, i)
                    if not head:
                        pe.wait_ge(scored, NB * i - NB)
                    for d in range(DB):
                        for c in range(NB):
                            last = pe.transpose(bank[4 + d][:, cols(c)], x1[:, c, cols(d)], ident[:, :])
                        last.then_inc(x1T_filled, 1)
                if prepare:
                    transpose_H(i + 1, 1)
                if tail:
                    if head:
                        pe.wait_ge(z_ready, NB * i + NB)
                    for d in range(DB):
                        pe.wait_ge(x1T_hi_ready, 2 * i - 1 + d)
                        for a in range(DB):
                            for w in (M_hi, M_lo):
                                pe.matmul(bank[2 + a][:, :], w[:, d, cols(a)], x1T_hi[:, d, :],
                                          start=(d == 0 and w is M_hi), stop=False)
                    pe.wait_ge(x1T_lo_ready, 2 * i)
                    for a in range(DB):
                        for d in range(DB):
                            last = pe.matmul(bank[2 + a][:, :], M_hi[:, d, cols(a)], x1T_lo[:, d, :],
                                             start=False, stop=(d == DB - 1))
                        last.then_inc(xmT_filled, 1)
                    for c in range(NB):
                        for s, w in ((x1T_hi, Wv_hi), (x1T_hi, Wv_lo), (x1T_lo, Wv_hi)):
                            for d in range(DB):
                                last = pe.matmul(bank[4 + c // 2][:, cols(c % 2, D)], s[:, d, cols(c)], w[:, d, :],
                                                 start=(d == 0 and s is x1T_hi and w is Wv_hi),
                                                 stop=(d == DB - 1 and s is x1T_lo))
                        if c % 2:
                            last.then_inc(v_filled, 1)
                def make_S(blocks):
                    for c in blocks:
                        if c >= 2:
                            pe.wait_ge(v_ready, 2 * i - 3 + c)
                        for s, r in ((xmT_hi, x1T_hi), (xmT_hi, x1T_lo), (xmT_lo, x1T_hi)):
                            if c == 0 and s is xmT_lo:
                                pe.wait_ge(xmT_lo_ready, 2 * i)
                            for d in range(DB):
                                last = pe.matmul(bank[S_bank[c]][:, :], s[:, d, cols(c)], r[:, d, :],
                                                 start=(d == 0 and s is xmT_hi and r is x1T_hi),
                                                 stop=(d == DB - 1 and s is xmT_lo))
                        last.then_inc(S_filled, 1)

                if tail:
                    pe.wait_ge(xmT_hi_ready, 2 * i)
                    make_S((0, 1))
                if head:
                    pe.wait_ge(n1_ready, i + 1)
                    pe.wait_ge(n1_end_ready, i + 1)
                    if prepare and tail:
                        pe.wait_ge(HT_ready, NB * i + 2 * NB)
                    for k, to in enumerate(n1T_bank):
                        for c in range(NB):
                            last = pe.transpose(bank[to][:, cols(c)], z[:, c, cols(k)], ident[:, :])
                        last.then_inc(n1T_filled, 1)
                if tail:
                    make_S((2, 3))

                def make_y1(c, blocks=range(HB)):
                    for k in blocks:
                        if c == 0:
                            pe.wait_ge(n1T_hi_ready, HB * i + k + 1)
                            pe.wait_ge(n1T_lo_ready, HB * i + k + 1)
                        for s, w in ((n1T_hi, W2T_hi), (n1T_hi, W2T_lo), (n1T_lo, W2T_hi)):
                            last = pe.matmul(bank[6 + c // 2][:, cols(c % 2, D)], s[:, k, cols(c)], w[:, k, :],
                                             start=(k == 0 and s is n1T_hi and w is W2T_hi),
                                             stop=(k == HB - 1 and s is n1T_lo))
                    if c % 2 and HB - 1 in blocks:
                        last.then_inc(y1_filled, 1)

                if head:
                    make_y1(0)
                if tail:
                    pe.wait_ge(w_ready, i)
                    for c in range(NB):
                        last = pe.transpose(bank[2][0:1, cols(c)], w_masked[:, c:c + 1], ident[:, :])
                    last.then_inc(w_filled, 1)
                if head:
                    make_y1(1)
                    make_y1(2)
                    make_y1(3, range(HB - 1))
                if tail:
                    pe.wait_ge(p_row_ready, i)
                if head:
                    make_y1(3, range(HB - 1, HB))
                if tail:
                    for c in range(NB):
                        last = pe.transpose(bank[3][:, c:c + 1], p_row[0:1, cols(c)], ident[0:1, 0:1])
                    last.then_inc(p_filled, 1)
                if isinstance(i, int) and i == 0:
                    pe.wait_ge(M_lo_ready, 1)
                    pe.wait_ge(w2beta_ready, 1)
                if prepare:
                    make_m1(i + 1, nq)

            def halves_of(part):
                return part.rearrange("p a (k d) -> p (a k) d", d=D)

            steps(pe, step)

        @block.scalar
        def _(act):
            def copy_HT(q, b, h):
                act.wait_ge(HT_filled, 2 * b + h + 1)
                HT_bank = HT_banks(b)
                for k in range(2):
                    act.activation(HT[q][:, 2 * h + k, :], HT_bank[h][:, cols(k, N)], ACT.Copy,
                                   accum_out=count[q][:, 2 * h + k:2 * h + k + 1]).then_inc(HT_ready, 1)

            def rounded(to, frm, filled, filled_at, ready):
                act.wait_ge(filled, filled_at)
                act.activation(to, frm, ACT.Copy).then_inc(ready, 1)

            def edges_hi(m_hi, q, filled, first_bank, b2, ready):
                for h in range(2):
                    act.wait_ge(filled, b2 + h + 1)
                    for k in range(2):
                        last = act.activation(m_hi[:, h, cols(k, D)], bank[first_bank + h][:, cols(k, D)], ACT.Identity,
                                              scale=Be[q][:, 2 * h + k:2 * h + k + 1], bias=0.0)
                    last.then_inc(ready, 1)

            def normalise(n, to, frm, blocks):
                for k in blocks:
                    last = act.activation(to[:, k, :], frm[:, k, :], ACT.Identity,
                                          scale=rstd[n][:, k:k + 1], bias=shift[n][:, k:k + 1])
                return last

            act.wait_ge(x_in[0], 16)
            act.activation(x_hi[:, :, :], x_raw[0][:, :, :], ACT.Copy).then_inc(x_hi_ready, 1)
            copy_HT(0, 0, 0)
            copy_HT(0, 0, 1)
            act.wait_ge(Be_ready, 1)
            edges_hi(m1_hi, 0, m1_filled, 0, 0, m1_hi_ready)
            for d in range(DB):
                rounded(W1T_hi[:, d, :], bank[2 + d][:, :], W1T_filled, d + 1, W1T_hi_ready)
            def split_W2():
                act.wait_ge(columns_loaded, 32)
                for h in range(2):
                    act.wait_ge(W2T_filled, h + 1)
                    for k in range(2 * h, 2 * h + 2):
                        act.activation(W2T_hi[:, k, :], bank[2 + h][:, cols(k % 2, D)], ACT.Identity,
                                       scale=gamma_col[:, k:k + 1], bias=0.0)
                    act.activation(W2T_f[:, 2 * h:2 * h + 2, :], halves(bank[2 + h][:, :]), ACT.Copy).then_inc(W2T_f_ready, 1)

            def set_up_products():
                rounded(M_hi[:, :, :], halves(bank[0][:, :]), M_filled, 1, M_hi_ready)
                act.wait_ge(w2beta_filled, 1)
                act.activation(w2beta[:, 0, :], bank[1][:, 0:D], ACT.Copy)
                act.activation(w2beta[:, 1, :], bank[1][:, 0:D], ACT.Copy).then_inc(w2beta_ready, 1)
                act.wait_ge(Wv_loaded, 16)
                act.activation(Wv_hi[:, :, :], Wv_in, ACT.Copy).then_inc(Wv_hi_ready, 1)

            def step(i, q, half, prepare, head, tail):
                nq = 1 - q
                if tail:
                    edges_hi(m2_hi, nq, m2_filled, 2, 2 * i - 2, m2_hi_ready)
                if isinstance(i, int) and i == B:
                    finish(i - 1)
                if head:
                    for d in range(DB):
                        rounded(gy_hi[:, d, :], bank[4 + d][:, :], g_filled, 2 * i + d + 1, g_hi_ready)

                def x_high():
                    act.wait_ge(m1_filled, 2 * i + 2)
                    act.wait_ge(x_in[nq], 16 * (half + q) + 16)
                    act.activation(x_hi[:, :, :], x_raw[nq][:, :, :], ACT.Copy).then_inc(x_hi_ready, 1)

                if prepare and tail:
                    x_high()
                if isinstance(i, int) and i == 0:
                    split_W2()
                    for h in range(2):
                        rounded(WqkT_f[:, 2 * h:2 * h + 2, :], halves(bank[6 + h][:, :]), WqkT_filled, h + 1, WqkT_f_ready)

                def copy_H():
                    act.wait_ge(H_bf_ready, NB * i + 2 * NB)
                    act.activation(H[nq][:, :, :], H_bf[:, :, :], ACT.Copy).then_inc(H_ready, 1)

                def relu(c):
                    act.wait_ge(z_ready, NB * i + c + 1)
                    act.activation(z[:, c, :], z[:, c, :], ACT.Relu).then_inc(relu_ready, 1)

                if head:
                    relu(0)
                if tail:
                    act.wait_ge(shift_ready[1], i)
                    normalise(1, x1, y2, (0, 1)).then_inc(x1_ready, 1)
                if head:
                    relu(1)
                if tail:
                    for d in range(DB):
                        rounded(x1T_hi[:, d, :], bank[4 + d][:, :], x1T_filled, 2 * i - 1 + d, x1T_hi_ready)
                if head:
                    relu(2)
                    relu(3)
                if prepare and tail:
                    copy_HT(nq, i + 1, 0)
                if tail:
                    for d in range(DB):
                        rounded(xmT_hi[:, d, :], bank[2 + d][:, :], xmT_filled, 2 * i - 1 + d, xmT_hi_ready)
                if prepare and tail:
                    copy_HT(nq, i + 1, 1)
                if tail:
                    rounded(v[:, 0, :], bank[4][:, :], v_filled, 2 * i - 1, v_ready)
                if head:
                    act.wait_ge(shift_ready[0], i + 1)
                    normalise(0, z, z, (0, 1)).then_inc(n1_ready, 1)
                if isinstance(i, int) and i == 0:
                    x_high()
                if tail:
                    rounded(v[:, 1, :], bank[5][:, :], v_filled, 2 * i, v_ready)
                if head:
                    for k, frm in enumerate(n1T_bank):
                        rounded(n1T_hi[:, k, :], bank[frm][:, :], n1T_filled, HB * i + k + 1, n1T_hi_ready)
                if isinstance(i, int) and i == 0:
                    set_up_products()
                    copy_HT(1, 1, 0)
                    copy_HT(1, 1, 1)
                if prepare:
                    copy_H()

                def y1_hi(h):
                    act.wait_ge(y1_ready, 2 * i + h + 1)
                    act.activation(gy_hi[:, h, :], y1[:, h, :], ACT.Copy).then_inc(y1_hi_ready, 1)

                if tail:
                    act.wait_ge(bias_ready, i)
                    act.activation(exps[0:1, :], bank[2][0:1, :], ACT.Exp, scale=SCALE, bias=w_bias[0:1, 0:1],
                                   accum_out=exp_sum[0:1, 0:1]).then_inc(exp_ready, 1)
                if head:
                    y1_hi(0)
                    y1_hi(1)
                if prepare:
                    act.wait_ge(Be_ready, i + 2)
                    edges_hi(m1_hi, nq, m1_filled, 0, 2 * i + 2, m1_hi_ready)
                if tail and not (isinstance(i, int) and i == B - 1):
                    finish(i)

            def finish(i):
                act.wait_ge(shift_ready[2], i)
                if not (isinstance(i, int) and i < 2):
                    act.wait_ge(stored, 16 * i - 16)
                normalise(2, result, y2, (0, 1)).then_inc(result_ready, 1)

            steps(act, step)

        @block.vector
        def _(dve):
            def lo_of(to, frm, hi, hi_ready, hi_at, ready):
                dve.wait_ge(hi_ready, hi_at)
                dve.tensor_tensor(to, frm, hi.bitcast(F32), ALU.subtract).then_inc(ready, 1)

            def edges_lo(m_lo, m_hi, q, first_bank, h, at, hi_ready, ready):
                dve.wait_ge(hi_ready, at)
                for k in range(2):
                    last = dve.scalar_tensor_tensor(m_lo[:, h, cols(k, D)], bank[first_bank + h][:, cols(k, D)],
                                                    Be[q][:, 2 * h + k:2 * h + k + 1],
                                                    m_hi[:, h, cols(k, D)].bitcast(F32), ALU.mult, ALU.subtract)
                last.then_inc(ready, 1)

            def make_H_bf(q, blocks):
                for c in blocks:
                    dve.tensor_scalar(H_bf[:, c, :], adj_raw[q][:, c, :], 0.0, None, ALU.not_equal).then_inc(H_bf_ready, 1)

            def normalise_end(n, to, frm):
                for k in (2, 3):
                    last = dve.tensor_scalar(to[:, k, :], frm[:, k, :], rstd[n][:, k:k + 1], shift[n][:, k:k + 1],
                                             ALU.mult, ALU.add)
                return last

            def guarded_inverse(to, frm, floor, scratch, frm_ready, frm_at, mid_ready, mid_at, ready):
                dve.wait_ge(frm_ready, frm_at)
                dve.tensor_scalar(scratch, frm, floor, None, ALU.max).then_inc(mid_ready, 1)
                dve.wait_ge(mid_ready, mid_at + 1)
                dve.reciprocal(to, scratch).then_inc(mid_ready, 1)
                dve.wait_ge(mid_ready, mid_at + 2)
                dve.scalar_tensor_tensor(to, frm, 0.0, to, ALU.is_gt, ALU.mult).then_inc(ready, 1)

            def make_Be(b, q):
                guarded_inverse(Be[q][:, :], count[q][:, :], 0.5, inv_count[:, :], HT_ready, NB * b + NB,
                                count_inv_ready, 2 * b, Be_ready)

            def sum_degree(q, blocks):
                for c in blocks:
                    dve.scalar_tensor_tensor(unused[:, (c + 2) % NB, :], adj_raw[q][:, c, :], 0.0, row0[q][:, :], ALU.not_equal,
                                             ALU.mult, accum_out=degree[:, c:c + 1]).then_inc(degree_ready, 1)

            def make_Dn(b, q):
                guarded_inverse(Dn[q][:, :], degree[:, :], TINY, inv_degree[:, :], degree_ready, NB * b + NB,
                                degree_inv_ready, 2 * b, Dn_ready)

            def take_stats(n, frm, k):
                dve.bn_stats(stats[n][:, k, :], frm[:, k, :]).then_inc(stats_ready[n], 1)

            def await_stats(n, b):
                dve.wait_ge(stats_ready[n], 4 * b + 4)

            def take_moments(n):
                for k in range(4):
                    last = dve.bn_aggr(moments[n][:, k, :], stats[n][:, k, :])
                last.then_inc(moments_ready[n], 1)

            def take_shift(n, b):
                dve.wait_ge(rstd_ready[n], b + 1)
                dve.scalar_tensor_tensor(shift[n][:, :], moments[n][:, :, 0], -1.0, rstd[n][:, :],
                                         ALU.mult, ALU.mult).then_inc(shift_ready[n], 1)

            dve.memset(ones[:, :], 1.0).then_inc(ones_ready, 1)
            dve.wait_ge(ident_ready, 1)
            dve.tensor_copy(ident_bf[:, :], ident[:, :]).then_inc(ident_bf_ready, 1)
            for c in range(NB):
                dve.wait_ge(first_adj_in[c], 16)
                make_H_bf(0, (c,))
                dve.tensor_scalar(H[0][:, c, :], adj_raw[0][:, c, :], 0.0, None, ALU.not_equal).then_inc(first_H_ready, 1)
            dve.wait_ge(row0_in[0], 16)
            sum_degree(0, range(2))
            make_Be(0, 0)
            dve.wait_ge(Be_ready, 1)
            for h in range(2):
                edges_lo(m1_lo, m1_hi, 0, 0, h, h + 1, m1_hi_ready, m1_lo_ready)
            for d in range(DB):
                lo_of(W1T_lo[:, d, :], bank[2 + d][:, :], W1T_hi[:, d, :], W1T_hi_ready, d + 1, W1T_lo_ready)
            sum_degree(0, range(2, NB))
            make_Dn(0, 0)
            dve.wait_ge(columns_loaded, 32)

            def spread_beta():
                dve.wait_ge(ones_ready, 1)
                for k in range(HB):
                    last = dve.tensor_scalar(beta_wide[:, k, :], ones[:, :], beta_col[:, k:k + 1], None, ALU.mult)
                last.then_inc(beta_ready, 1)

            def split_W2():
                for h in range(2):
                    dve.wait_ge(W2T_f_ready, h + 1)
                    for k in range(2 * h, 2 * h + 2):
                        last = dve.scalar_tensor_tensor(W2T_lo[:, k, :], bank[2 + h][:, cols(k % 2, D)],
                                                        gamma_col[:, k:k + 1], W2T_hi[:, k, :].bitcast(F32),
                                                        ALU.mult, ALU.subtract)
                    last.then_inc(W2T_lo_ready, 1)

            def step(i, q, half, prepare, head, tail):
                nq = 1 - q
                if tail:
                    edges_lo(m2_lo, m2_hi, nq, 2, 0, 2 * i - 1, m2_hi_ready, m2_lo_ready)
                    edges_lo(m2_lo, m2_hi, nq, 2, 1, 2 * i, m2_hi_ready, m2_lo_ready)
                if isinstance(i, int) and i == B:
                    finish(i - 1)
                if prepare and tail:
                    dve.wait_ge(adj_in[nq], adj_count(half + q, nq))
                    make_H_bf(nq, (0, 1))
                if head:
                    for d in range(DB):
                        lo_of(gy_lo[:, d, :], bank[4 + d][:, :], gy_hi[:, d, :], g_hi_ready, 2 * i + d + 1, g_lo_ready)
                if isinstance(i, int) and i == 0:
                    split_W2()
                if prepare and tail:
                    make_H_bf(nq, (2,))
                if tail:
                    dve.wait_ge(base_ready, i)
                    if not (isinstance(i, int) and i < 2):
                        dve.wait_ge(result_ready, i - 1)
                    for h in range(2):
                        dve.wait_ge(y2_filled, 2 * i - 1 + h)
                        for c in range(2 * h, 2 * h + 2):
                            last = dve.scalar_tensor_tensor(y2[:, c, :], bank[6 + h][:, cols(c % 2, D)],
                                                            Dn[nq][:, c:c + 1], base[:, c, :], ALU.mult, ALU.add)
                        last.then_inc(y2_ready, 1)
                        dve.wait_ge(y2_ready, 2 * i - 1 + h)
                        for c in range(2 * h, 2 * h + 2):
                            take_stats(1, y2, c)
                    await_stats(1, i - 1)
                if prepare and tail:
                    make_H_bf(nq, (3,))
                if tail:
                    take_moments(1)

                def make_z(c):
                    dve.wait_ge(z_filled, NB * i + c + 1)
                    dve.scalar_tensor_tensor(z[:, c, :], bank[c][:, :], Dn[q][:, c:c + 1], b1_row[:, :],
                                             ALU.mult, ALU.add).then_inc(z_ready, 1)

                def relu_stats(c):
                    dve.wait_ge(relu_ready, NB * i + c + 1)
                    take_stats(0, z, c)

                if head:
                    dve.wait_ge(Dn_ready, i + 1)
                    if isinstance(i, int) and i == 0:
                        dve.wait_ge(rows_loaded, 48)
                    make_z(0)
                    make_z(1)
                if tail:
                    take_shift(1, i - 1)
                    dve.wait_ge(shift_ready[1], i)
                    normalise_end(1, x1, y2).then_inc(x1_end_ready, 1)
                if head:
                    relu_stats(0)
                    make_z(2)
                    make_z(3)
                    relu_stats(1)
                if tail:
                    lo_of(x1T_lo[:, 0, :], bank[4][:, :], x1T_hi[:, 0, :], x1T_hi_ready, 2 * i - 1, x1T_lo_ready)
                    lo_of(x1T_lo[:, 1, :], bank[5][:, :], x1T_hi[:, 1, :], x1T_hi_ready, 2 * i, x1T_lo_ready)
                if head:
                    relu_stats(2)
                    relu_stats(3)
                    await_stats(0, i)
                if tail:
                    lo_of(xmT_lo[:, 0, :], bank[2][:, :], xmT_hi[:, 0, :], xmT_hi_ready, 2 * i - 1, xmT_lo_ready)
                if head:
                    take_moments(0)
                if isinstance(i, int) and i == 0:
                    spread_beta()
                    dve.wait_ge(adj_in[nq], adj_count(half + q, nq))
                    make_H_bf(nq, range(NB))
                if tail:
                    lo_of(xmT_lo[:, 1, :], bank[3][:, :], xmT_hi[:, 1, :], xmT_hi_ready, 2 * i, xmT_lo_ready)
                if head:
                    take_shift(0, i)
                    dve.wait_ge(shift_ready[0], i + 1)
                    normalise_end(0, z, z).then_inc(n1_end_ready, 1)
                if prepare:
                    dve.wait_ge(row0_in[nq], 16 * (half + q) + 16)
                    sum_degree(nq, (0,))

                def score(c):
                    dve.wait_ge(S_filled, NB * i - NB + c + 1)
                    dve.tensor_tensor_reduce(out=unused[:, c, :], in0=bank[S_bank[c]][:, :], in1=adj_masked[nq][:, c, :],
                                             scale=1.0, scalar=0.0, op0=ALU.mult, op1=ALU.add,
                                             accum_out=w_sum[:, c:c + 1]).then_inc(scored, 1)

                if tail:
                    dve.wait_ge(masked_ready, NB * i)
                    score(0)
                if prepare:
                    sum_degree(nq, (1,))
                if tail:
                    score(1)
                if head:
                    for k, frm in enumerate(n1T_bank):
                        lo_of(n1T_lo[:, k, :], bank[frm][:, :], n1T_hi[:, k, :], n1T_hi_ready, HB * i + k + 1, n1T_lo_ready)
                if isinstance(i, int) and i == 0:
                    lo_of(M_lo[:, :, :], halves(bank[0][:, :]), M_hi[:, :, :], M_hi_ready, 1, M_lo_ready)
                    lo_of(Wv_lo[:, :, :], Wv_in, Wv_hi[:, :, :], Wv_hi_ready, 1, Wv_lo_ready)
                    dve.wait_ge(w2beta_ready, 1)
                if tail:
                    if prepare:
                        dve.wait_ge(degree_ready, NB * i + NB + 2)
                    score(2)
                    score(3)
                    dve.wait_ge(scored, NB * i)
                    dve.tensor_tensor(w_masked[:, :], w_sum[:, :], mask_col[:, i - 1, :], ALU.mult).then_inc(w_ready, 1)
                if prepare:
                    make_Be(i + 1, nq)

                def make_y1(h):
                    dve.wait_ge(y1_filled, 2 * i + h + 1)
                    dve.tensor_tensor(y1[:, h, :], bank[6 + h][:, :], w2beta[:, :, :].rearrange("p a d -> p (a d)"),
                                      ALU.add).then_inc(y1_ready, 1)

                if tail:
                    dve.wait_ge(w_filled, i)
                    dve.tensor_reduce(w_max[:, :], bank[2][0:1, :], AX_X, ALU.max).then_inc(max_ready, 1)
                    dve.wait_ge(max_ready, i)
                    dve.tensor_scalar(w_bias[:, :], w_max[:, :], -SCALE, None, ALU.mult).then_inc(bias_ready, 1)
                if head:
                    make_y1(0)
                if tail:
                    dve.wait_ge(exp_ready, i)
                    dve.reciprocal(exp_inv[:, :], exp_sum[:, :]).then_inc(exp_inv_ready, 1)
                    dve.wait_ge(exp_inv_ready, i)
                    dve.tensor_scalar(p_row[:, :], exps[:, :], exp_inv[:, :], None, ALU.mult).then_inc(p_row_ready, 1)

                def make_y3(c):
                    dve.scalar_tensor_tensor(y2[:, c, :], v[:, c // 2, cols(c % 2, D)], p_col[:, c:c + 1],
                                             x1[:, c, :], ALU.mult, ALU.add).then_inc(y3_ready, 1)

                if prepare:
                    sum_degree(nq, (2, 3))
                if head:
                    make_y1(1)
                if tail:
                    dve.wait_ge(p_filled, i)
                    dve.tensor_copy(p_col[:, :], bank[3][:, 0:NB]).then_inc(p_ready, 1)
                    dve.wait_ge(p_ready, i)
                    make_y3(0)
                if isinstance(i, int) and i == B - 1:
                    for h in range(2):
                        lo_of(gy_lo[:, h, :], y1[:, h, :], gy_hi[:, h, :], y1_hi_ready, 2 * i + h + 1, y1_lo_ready)
                if tail:
                    make_y3(1)
                    make_y3(2)
                    make_y3(3)
                    for c in range(NB):
                        dve.wait_ge(y3_ready, NB * i - NB + c + 1)
                        take_stats(2, y2, c)
                    await_stats(2, i - 1)
                if prepare:
                    edges_lo(m1_lo, m1_hi, nq, 0, 0, 2 * i + 3, m1_hi_ready, m1_lo_ready)
                if tail:
                    take_moments(2)
                if prepare:
                    edges_lo(m1_lo, m1_hi, nq, 0, 1, 2 * i + 4, m1_hi_ready, m1_lo_ready)
                    make_Dn(i + 1, nq)
                if tail and not (isinstance(i, int) and i == B - 1):
                    finish(i)

            def finish(i):
                take_shift(2, i - 1)
                dve.wait_ge(shift_ready[2], i)
                if not (isinstance(i, int) and i < 2):
                    dve.wait_ge(stored, 16 * i - 16)
                normalise_end(2, result, y2).then_inc(result_end_ready, 1)

            steps(dve, step)

        @block.gpsimd
        def _(pool):
            def x_low(b, q):
                pool.wait_ge(x_hi_ready, b + 1)
                pool.tensor_tensor(x_lo[:, :, :], x_raw[q][:, :, :], x_hi[:, :, :].bitcast(F32),
                                   ALU.subtract).then_inc(x_lo_ready, 1)

            def inverse_std(n, b):
                pool.wait_ge(moments_ready[n], b + 1)
                pool.tensor_tensor(varp[n][:, :], moments[n][:, :, 1], eps_col[:, :], ALU.add)\
                    .then_inc(varp_ready[n], 1)
                pool.wait_ge(varp_ready[n], b + 1)
                pool.tensor_tensor(rstd[n][:, :], varp[n][:, :], minus_half[:, :], ALU.pow).then_inc(rstd_ready[n], 1)

            pool.memset(minus_half[:, :], -0.5).then_inc(half_ready, 1)
            pool.memset(eps_col[:, :], EPS).then_inc(half_ready, 1)
            pool.memset(ident[:, :], 0.0).then_inc(ident_zero, 1)
            pool.wait_ge(ident_zero, 1)
            pool.affine_select(out=ident[:, :], in_=ident[:, :], compare_op=ALU.not_equal, fill=1.0, base=0,
                               pattern=[[-1, P]], channel_multiplier=1).then_inc(ident_ready, 1)
            x_low(0, 0)
            pool.wait_ge(half_ready, 2)

            def step(i, q, half, prepare, head, tail):
                nq = 1 - q
                if head:
                    pool.wait_ge(maskrow_in[q], 16 * half + 16)
                    if isinstance(i, int) and i == 0:
                        for c in range(NB):
                            pool.wait_ge(first_adj_in[c], 16)
                    else:
                        pool.wait_ge(adj_in[q], adj_count(half, q))
                    if not (isinstance(i, int) and i < 2):
                        pool.wait_ge(scored, NB * i - NB)
                    for c in range(NB):
                        pool.tensor_tensor(adj_masked[q][:, c, :].rearrange("p (k n) -> p k n", k=NB),
                                           adj_raw[q][:, c, :].rearrange("p (n k) -> p k n", k=NB),
                                           maskrow[q][:, :].rearrange("p (n k) -> p k n", k=NB),
                                           ALU.mult).then_inc(masked_ready, 1)
                if isinstance(i, int) and i == 0:
                    inverse_std(0, 0)
                if prepare:
                    x_low(i + 1, nq)
                if isinstance(i, int) and i == 0:
                    pool.wait_ge(rows_loaded, 48)
                if tail:
                    inverse_std(1, i - 1)
                if head:
                    if tail:
                        pool.wait_ge(y2_ready, 2 * i)
                    pool.tensor_tensor(base[:, :, :], x_raw[q][:, :, :], x_raw[q][:, :, :], ALU.add)\
                        .then_inc(twice_ready, 1)
                    pool.wait_ge(twice_ready, i + 1)
                    pool.tensor_tensor(base[:, :, :], base[:, :, :],
                                       b2_row[:, :].rearrange("p (a d) -> p a d", a=1).to_broadcast([P, NB, D]),
                                       ALU.add).then_inc(base_ready, 1)
                if head and tail:
                    inverse_std(0, i)

                def y1_low(h):
                    pool.wait_ge(y1_hi_ready, 2 * i + h + 1)
                    pool.tensor_tensor(gy_lo[:, h, :], y1[:, h, :], gy_hi[:, h, :].bitcast(F32),
                                       ALU.subtract).then_inc(y1_lo_ready, 1)

                if head and not (isinstance(i, int) and i == B - 1):
                    y1_low(0)
                    y1_low(1)
                if tail:
                    inverse_std(2, i - 1)

            steps(pool, step)


_INS = ['x', 'adj', 'nodemask', 'L0_gnn_W1', 'L0_gnn_b1', 'L0_gnn_gamma', 'L0_gnn_beta', 'L0_gnn_W2', 'L0_gnn_b2',
        'L1_gnn_Wqk', 'L1_gnn_Wv']


def kernel(**inputs):
    import numpy as _np
    import concourse.bacc as _bacc
    from concourse import mybir as _mybir
    from concourse.bass_utils import run_bass_kernel_spmd as _run

    nc = _bacc.Bacc("TRN2", target_bir_lowering=False, num_devices=1)
    arrays, args = {}, []
    for name in _INS:
        a = _np.ascontiguousarray(inputs[name])
        arrays[f"in_{name}_dram"] = a
        args.append(nc.dram_tensor(f"in_{name}_dram", a.shape, _mybir.dt.from_np(a.dtype), kind="ExternalInput").ap())
    shape = inputs['x'].shape
    args.append(nc.dram_tensor("out_dram", shape, _mybir.dt.from_np(_np.dtype('float32')), kind="ExternalOutput").ap())
    graph_kernel(nc, *args)
    r = _run(nc, [arrays], core_ids=[0])
    return r.results[0]["out_dram"]
```

```python
from contextlib import ExitStack

import concourse.bass as bass
from concourse import mybir

P = 128
F32 = mybir.dt.float32
F32R = mybir.dt.float32r
BF16 = mybir.dt.bfloat16
ALU = mybir.AluOpType
ACT = mybir.ActivationFunctionType
AX_X = mybir.AxisListType.X
EPS = 1e-5
TINY = 1.17549435e-38



def graph_kernel(nc, x, adj, nodemask, W1, b1, gamma, beta, W2, b2, Wqk, Wv, out):
    B, N, D = x.shape
    HID = W1.shape[0]
    NB = N // P
    DB = D // P
    HB = HID // P
    BANK = 512
    assert NB == 4 and DB == 2 and HB == 4 and N == BANK and HID == BANK and Wqk.shape[1] == 2 * D
    SCALE = float(D) ** -0.5
    WARMING = 18

    with ExitStack() as ctx:
        def sb(name, shape, dt=F32):
            return ctx.enter_context(nc.sbuf_tensor(name, shape, dt))

        def sem(name):
            return ctx.enter_context(nc.semaphore(name))

        bank = [ctx.enter_context(nc.psum_tensor(f"bank{i}", [P, BANK], F32)) for i in range(8)]

        def HT_banks(b):
            first = 4 if isinstance(b, int) and b == 1 else 6
            return [bank[first + h][:, :].bitcast(BF16) for h in range(2)]

        S_bank = (0, 1, 4, 5)
        n1T_bank = (6, 7, 2, 3)


        adj_raw = [sb(f"adj_raw{q}", [P, NB, N]) for q in range(2)]
        adj_masked = [sb(f"adj_masked{q}", [P, NB, N]) for q in range(2)]
        x_raw = [sb(f"x_raw{q}", [P, NB, D]) for q in range(2)]
        H = [sb(f"H{q}", [P, NB, N], F32R) for q in range(2)]
        H_bf = sb("H_bf", [P, NB, N], BF16)
        HT = [sb(f"HT{q}", [P, NB, N], F32R) for q in range(2)]
        row0 = [sb(f"row0_{q}", [P, N]) for q in range(2)]
        maskrow = [sb(f"maskrow{q}", [P, N]) for q in range(2)]
        count = [sb(f"count{q}", [P, NB]) for q in range(2)]
        Be = [sb(f"Be{q}", [P, NB]) for q in range(2)]
        Dn = [sb(f"Dn{q}", [P, NB]) for q in range(2)]
        x_hi = sb("x_hi", [P, NB, D], F32R)
        x_lo = sb("x_lo", [P, NB, D], F32R)
        base = sb("base", [P, NB, D])
        wide = sb("wide", [P, 2, NB, N], F32R)
        m1_hi, m1_lo = wide[:, 0, 0:2, :], wide[:, 0, 2:4, :]
        m2_hi, m2_lo = wide[:, 1, 0:2, :], wide[:, 1, 2:4, :]
        n1T_hi, n1T_lo = wide[:, 0], wide[:, 1]
        gy = sb("gy", [P, 2, 2, BANK], F32R)
        gy_hi, gy_lo = gy[:, 0], gy[:, 1]
        z = sb("z", [P, NB, HID])
        y1 = sb("y1", [P, 2, BANK])
        y2 = sb("y2", [P, NB, D])
        x1 = sb("x1", [P, NB, D])
        x1T_hi = sb("x1T_hi", [P, DB, N], F32R)
        x1T_lo = sb("x1T_lo", [P, DB, N], F32R)
        xmT_hi = sb("xmT_hi", [P, DB, N], F32R)
        xmT_lo = sb("xmT_lo", [P, DB, N], F32R)
        v = sb("v", [P, 2, BANK])
        result = sb("result", [P, NB, D])
        unused = sb("unused", [P, NB, N])
        exps, p_row = sb("exps", [1, N]), sb("p_row", [1, N])
        degree = sb("degree", [P, NB])
        inv_count, inv_degree = sb("inv_count", [P, NB]), sb("inv_degree", [P, NB])
        stats = [sb(f"stats{n}", [P, 4, 6]) for n in range(3)]
        moments = [sb(f"moments{n}", [P, 4, 2]) for n in range(3)]
        varp = [sb(f"varp{n}", [P, 4]) for n in range(3)]
        rstd = [sb(f"rstd{n}", [P, 4]) for n in range(3)]
        shift = [sb(f"shift{n}", [P, 4]) for n in range(3)]
        minus_half, eps_col = sb("minus_half", [P, 4]), sb("eps_col", [P, 4])
        w_sum, w_masked, p_col = sb("w_sum", [P, NB]), sb("w_masked", [P, NB]), sb("p_col", [P, NB])
        w_max, w_bias = sb("w_max", [1, 1]), sb("w_bias", [1, 1])
        exp_sum, exp_inv = sb("exp_sum", [1, 1]), sb("exp_inv", [1, 1])
        ident, ident_bf, ones = sb("ident", [P, P]), sb("ident_bf", [P, P], BF16), sb("ones", [P, P])
        mask_col = sb("mask_col", [P, B, NB])
        b1_row, b2_row = sb("b1_row", [P, HID]), sb("b2_row", [P, D])
        gamma_col, beta_col = sb("gamma_col", [P, HB]), sb("beta_col", [P, HB])
        W1T_hi, W1T_lo = sb("W1T_hi", [P, DB, HID], F32R), sb("W1T_lo", [P, DB, HID], F32R)
        W2T_hi, W2T_lo = sb("W2T_hi", [P, HB, D], F32R), sb("W2T_lo", [P, HB, D], F32R)
        M_hi, M_lo = sb("M_hi", [P, DB, D], F32R), sb("M_lo", [P, DB, D], F32R)
        Wv_hi, Wv_lo = sb("Wv_hi", [P, DB, D], F32R), sb("Wv_lo", [P, DB, D], F32R)
        w2beta = sb("w2beta", [P, 2, D])
        W1_in = z[:, 0:2, :].rearrange("p a n -> p (a n)").rearrange("p (k d) -> p k d", d=D)
        Wqk_in = z[:, 2:4, :]
        W2_in = v[:, :, :]
        Wv_in = result[:, 0:2, :]
        W2T_f = x1[:, :, :].rearrange("p a n -> p (a n)").rearrange("p (k d) -> p k d", d=D)
        WqkT_f = y2[:, :, :].rearrange("p a n -> p (a n)").rearrange("p (k d) -> p k d", d=D)
        beta_wide = y1[:, :, :].rearrange("p a n -> p (a n)")[:, 0:HB * P].rearrange("p (k n) -> p k n", n=P)

        adj_in = [sem(f"adj_in{q}") for q in range(2)]
        first_adj_in = [sem(f"first_adj_in{c}") for c in range(NB)]
        x_in = [sem(f"x_in{q}") for q in range(2)]
        row0_in = [sem(f"row0_in{q}") for q in range(2)]
        maskrow_in = [sem(f"maskrow_in{q}") for q in range(2)]
        W1_loaded, W2_loaded, Wqk_loaded = sem("W1_loaded"), sem("W2_loaded"), sem("Wqk_loaded")
        Wv_loaded, columns_loaded, rows_loaded = sem("Wv_loaded"), sem("columns_loaded"), sem("rows_loaded")
        stored = sem("stored")
        HT_filled, m1_filled, m2_filled, g_filled = sem("HT_filled"), sem("m1_filled"), sem("m2_filled"), sem("g_filled")
        y2_filled, z_filled, x1T_filled = sem("y2_filled"), sem("z_filled"), sem("x1T_filled")
        xmT_filled, v_filled, n1T_filled = sem("xmT_filled"), sem("v_filled"), sem("n1T_filled")
        S_filled, y1_filled, w_filled, p_filled = sem("S_filled"), sem("y1_filled"), sem("w_filled"), sem("p_filled")
        x_hi_ready, m1_hi_ready = sem("x_hi_ready"), sem("m1_hi_ready")
        m2_hi_ready, g_hi_ready = sem("m2_hi_ready"), sem("g_hi_ready")
        relu_ready, x1_ready, HT_ready = sem("relu_ready"), sem("x1_ready"), sem("HT_ready")
        x1T_hi_ready, xmT_hi_ready, v_ready = sem("x1T_hi_ready"), sem("xmT_hi_ready"), sem("v_ready")
        n1_ready, n1T_hi_ready, exp_ready = sem("n1_ready"), sem("n1T_hi_ready"), sem("exp_ready")
        y1_hi_ready, result_ready = sem("y1_hi_ready"), sem("result_ready")
        first_H_ready = sem("first_H_ready")
        H_ready, H_bf_ready, Be_ready, Dn_ready = sem("H_ready"), sem("H_bf_ready"), sem("Be_ready"), sem("Dn_ready")
        m1_lo_ready, m2_lo_ready, g_lo_ready = sem("m1_lo_ready"), sem("m2_lo_ready"), sem("g_lo_ready")
        y2_ready, z_ready, x1T_lo_ready = sem("y2_ready"), sem("z_ready"), sem("x1T_lo_ready")
        xmT_lo_ready, n1T_lo_ready, scored = sem("xmT_lo_ready"), sem("n1T_lo_ready"), sem("scored")
        w_ready, y1_ready, bias_ready = sem("w_ready"), sem("y1_ready"), sem("bias_ready")
        exp_inv_ready, p_row_ready = sem("exp_inv_ready"), sem("p_row_ready")
        p_ready, y3_ready = sem("p_ready"), sem("y3_ready")
        x1_end_ready, n1_end_ready, result_end_ready = sem("x1_end_ready"), sem("n1_end_ready"), sem("result_end_ready")
        max_ready, degree_ready = sem("max_ready"), sem("degree_ready")
        count_inv_ready, degree_inv_ready = sem("count_inv_ready"), sem("degree_inv_ready")
        stats_ready = [sem(f"stats_ready{n}") for n in range(3)]
        moments_ready = [sem(f"moments_ready{n}") for n in range(3)]
        shift_ready = [sem(f"shift_ready{n}") for n in range(3)]
        x_lo_ready, y1_lo_ready, masked_ready = sem("x_lo_ready"), sem("y1_lo_ready"), sem("masked_ready")
        base_ready, twice_ready = sem("base_ready"), sem("twice_ready")
        varp_ready = [sem(f"varp_ready{n}") for n in range(3)]
        rstd_ready = [sem(f"rstd_ready{n}") for n in range(3)]
        ident_zero, ident_ready, ident_bf_ready = sem("ident_zero"), sem("ident_ready"), sem("ident_bf_ready")
        half_ready, ones_ready = sem("half_ready"), sem("ones_ready")
        beta_ready, W1T_filled, W2T_filled = sem("beta_ready"), sem("W1T_filled"), sem("W2T_filled")
        WqkT_filled, w2beta_filled, M_filled = sem("WqkT_filled"), sem("w2beta_filled"), sem("M_filled")
        W1T_hi_ready, W2T_f_ready, WqkT_f_ready = sem("W1T_hi_ready"), sem("W2T_f_ready"), sem("WqkT_f_ready")
        M_hi_ready, Wv_hi_ready, w2beta_ready = sem("M_hi_ready"), sem("Wv_hi_ready"), sem("w2beta_ready")
        W1T_lo_ready, W2T_lo_ready = sem("W1T_lo_ready"), sem("W2T_lo_ready")
        M_lo_ready, Wv_lo_ready = sem("M_lo_ready"), sem("Wv_lo_ready")

        block = ctx.enter_context(nc.Block())

        def cols(k, n=P):
            return slice(k * n, (k + 1) * n)

        def adj_count(half, q):
            return 16 * half if q == 0 else 16 * half + 16

        def halves(bank_ap):
            return bank_ap.rearrange("p (k d) -> p k d", d=D)

        def x1_of(i):
            return z[:, :, D:2 * D] if isinstance(i, int) and i == B else x1

        def y2_of(i):
            return z[:, :, 0:D] if isinstance(i, int) and i == B else y2

        def w_bank(i):
            return 0 if isinstance(i, int) and i == B - 1 else 2

        def p_bank(i):
            return 1 if isinstance(i, int) and i == B - 1 else 3

        def steps(engine, step, last_step):
            step(0, 0, 0, True, False, False)
            step(1, 1, 0, True, True, True)
            with engine.Fori(1, B // 2 - 1) as t:
                step(2 * t, 0, t, True, True, True)
                step(2 * t + 1, 1, t, True, True, True)
            step(B - 2, 0, B // 2 - 1, True, True, True)
            step(B - 1, 1, B // 2 - 1, False, True, False)
            last_step()

        x_dram = x.rearrange("b (p k) d -> b p k d", k=NB)
        adj_dram = adj.rearrange("b (p k) e -> b p k e", k=NB)
        adj_rows, mask_rows = adj, nodemask.rearrange("b (a n) -> b a n", a=1)
        out_dram = out.rearrange("b (p k) d -> b p k d", k=NB)

        @block.sync
        def _(sp):
            def load(b, q):
                sp.dma_start(adj_raw[q][:, :, :], adj_dram[b]).then_inc(adj_in[q], 16)
                sp.dma_start(x_raw[q][:, :, :], x_dram[b]).then_inc(x_in[q], 16)
                sp.dma_start(row0[q][:, :], adj_rows[b, 0:1, :].to_broadcast([P, N])).then_inc(row0_in[q], 16)
                sp.dma_start(maskrow[q][:, :], mask_rows[b].to_broadcast([P, N])).then_inc(maskrow_in[q], 16)

            sp.dma_start(x_raw[0][:, :, :], x_dram[0]).then_inc(x_in[0], 16)
            for c in range(NB):
                sp.dma_start(adj_raw[0][:, c, :], adj_dram[0][:, c, :]).then_inc(first_adj_in[c], 16)
            sp.dma_start(row0[0][:, :], adj_rows[0, 0:1, :].to_broadcast([P, N])).then_inc(row0_in[0], 16)
            sp.dma_start(maskrow[0][:, :], mask_rows[0].to_broadcast([P, N])).then_inc(maskrow_in[0], 16)
            sp.dma_start(W1_in, W1.rearrange("(k p) d -> p k d", p=P)).then_inc(W1_loaded, 16)
            sp.dma_start(W2_in, W2.rearrange("(k p) h -> p k h", p=P)).then_inc(W2_loaded, 16)
            with nc.allow_non_contiguous_dma(reason="two columns of 512 numbers, once"):
                sp.dma_start(gamma_col[:, :], gamma.rearrange("(k p) -> p k", p=P)).then_inc(columns_loaded, 16)
                sp.dma_start(beta_col[:, :], beta.rearrange("(k p) -> p k", p=P)).then_inc(columns_loaded, 16)
            sp.dma_start(Wqk_in, Wqk.rearrange("(k p) a -> p k a", p=P)).then_inc(Wqk_loaded, 16)
            sp.dma_start(b1_row[:, :], b1.rearrange("(a h) -> a h", a=1).to_broadcast([P, HID])).then_inc(rows_loaded, 16)
            sp.dma_start(b2_row[:, :], b2.rearrange("(a d) -> a d", a=1).to_broadcast([P, D])).then_inc(rows_loaded, 16)
            sp.dma_start(mask_col[:, :, :], nodemask.rearrange("b (p k) -> p b k", k=NB)).then_inc(rows_loaded, 16)
            load(1, 1)
            sp.dma_start(Wv_in, Wv.rearrange("(k p) d -> p k d", p=P)).then_inc(Wv_loaded, 16)

            def step(i, q, half, prepare, tail, scores):
                if prepare and not (isinstance(i, int) and i + 2 >= B):
                    if isinstance(i, int) and i == 0:
                        sp.wait_ge(first_H_ready, NB)
                    sp.wait_ge(x_hi_ready, i + 1)
                    sp.wait_ge(H_bf_ready, NB * i + NB)
                    sp.wait_ge(degree_ready, NB * i + NB)
                    sp.wait_ge(masked_ready, NB * i + NB)
                    sp.wait_ge(x_lo_ready, i + 1)
                    sp.wait_ge(base_ready, i + 1)
                    load(i + 2, q)
                if scores:
                    store(i)

            def store(i):
                sp.wait_ge(result_ready, i)
                sp.wait_ge(result_end_ready, i)
                sp.dma_start(out_dram[i - 1], result[:, :, :]).then_inc(stored, 16)

            def last_step():
                store(B - 1)
                store(B)

            steps(sp, step, last_step)
            sp.wait_ge(stored, 16 * B)

        @block.tensor
        def _(pe):
            def transpose_H(b, h):
                for k in range(2):
                    for c in range(NB):
                        last = pe.transpose(HT_banks(b)[h][:, cols(NB * k + c)], H_bf[:, c, cols(2 * h + k)], ident_bf[:, :])
                last.then_inc(HT_filled, 1)

            def gather_edges(q, hi, lo, banks, filled):
                for k in range(NB):
                    for c in range(NB):
                        for part in (hi, lo):
                            last = pe.matmul(bank[banks[k // 2]][:, cols(k % 2, D)], H[q][:, c, cols(k)], part[:, c, :],
                                             start=(c == 0 and part is hi), stop=(c == NB - 1 and part is lo))
                    if k % 2:
                        last.then_inc(filled, 1)

            def make_m1(n, q):
                if isinstance(n, int) and n == 0:
                    pe.wait_ge(first_H_ready, NB)
                else:
                    pe.wait_ge(H_ready, n)
                pe.wait_ge(x_hi_ready, n + 1)
                pe.wait_ge(x_lo_ready, n + 1)
                gather_edges(q, x_hi, x_lo, (0, 1), m1_filled)

            pe.wait_ge(ident_ready, 1)
            for k in range(WARMING):
                pe.transpose(bank[0][:, cols(k % 4)], ident[:, :], ident[:, :])
            pe.wait_ge(ident_bf_ready, 1)
            for c in range(NB):
                pe.wait_ge(H_bf_ready, c + 1)
                for e in range(NB):
                    last = pe.transpose(HT_banks(0)[e // 2][:, cols(NB * (e % 2) + c)], H_bf[:, c, cols(e)], ident_bf[:, :])
                    if c == NB - 1 and e % 2:
                        last.then_inc(HT_filled, 1)
            make_m1(0, 0)
            pe.wait_ge(W1_loaded, 16)
            for d in range(DB):
                for k in range(HB):
                    last = pe.transpose(bank[2 + d][:, cols(k)], W1_in[:, k, cols(d)], ident[:, :])
                last.then_inc(W1T_filled, 1)
            pe.wait_ge(HT_ready, NB)
            pe.wait_ge(W2_loaded, 16)
            for k in range(HB):
                for d in range(DB):
                    last = pe.transpose(bank[6 + k // 2][:, (k % 2) * D + d * P:(k % 2) * D + (d + 1) * P],
                                        W2_in[:, d, cols(k)], ident[:, :])
                if k % 2:
                    last.then_inc(W2T_filled, 1)

            def transpose_Wqk():
                pe.wait_ge(Wqk_loaded, 16)
                pe.wait_ge(W1T_lo_ready, 2)
                for k in range(4):
                    for d in range(DB):
                        last = pe.transpose(bank[2 + k // 2][:, (k % 2) * D + d * P:(k % 2) * D + (d + 1) * P],
                                            Wqk_in[:, d, cols(k)], ident[:, :])
                    if k % 2:
                        last.then_inc(WqkT_filled, 1)

            def set_up_products():
                pe.wait_ge(WqkT_f_ready, 2)
                pe.wait_ge(z_ready, 2)
                for d in range(DB):
                    for a in range(2):
                        last = pe.matmul(bank[0][:, cols(d, D)], WqkT_f[:, a, cols(d)], WqkT_f[:, 2 + a, :],
                                         start=(a == 0), stop=(a == 1))
                last.then_inc(M_filled, 1)
                pe.wait_ge(W2T_f_ready, 2)
                pe.wait_ge(beta_ready, 1)
                for k in range(HB):
                    last = pe.matmul(bank[1][:, 0:D], beta_wide[:, k, :], W2T_f[:, k, :],
                                     start=(k == 0), stop=(k == HB - 1))
                last.then_inc(w2beta_filled, 1)

            def halves_of(part):
                return part.rearrange("p a (k d) -> p (a k) d", d=D)

            def make_m2(i, q):
                pe.wait_ge(y1_hi_ready, 2 * i)
                pe.wait_ge(y1_lo_ready, 2 * i)
                if not (isinstance(i, int) and i < 2):
                    before = i - 2 if isinstance(i, int) and i == B else i - 1
                    pe.wait_ge(exp_ready, before)
                    pe.wait_ge(p_ready, before)
                gather_edges(q, halves_of(gy_hi), halves_of(gy_lo), (2, 3), m2_filled)

            def make_g(i, q, tail):
                pe.wait_ge(m1_lo_ready, 2 * i + 2)
                pe.wait_ge(HT_ready, NB * i + NB)
                if tail and not (isinstance(i, int) and i < 2):
                    pe.wait_ge(scored, NB * i - NB)
                for d in range(DB):
                    for e in range(NB):
                        for part in (m1_hi, m1_lo):
                            last = pe.matmul(bank[4 + d][:, :], halves_of(part)[:, e, cols(d)], HT[q][:, e, :],
                                             start=(e == 0 and part is m1_hi), stop=(e == NB - 1 and part is m1_lo))
                    last.then_inc(g_filled, 1)

            def make_y2(i, q):
                pe.wait_ge(m2_lo_ready, 2 * i)
                for c in range(NB):
                    for e in range(NB):
                        for part in (m2_hi, m2_lo):
                            last = pe.matmul(bank[6 + c // 2][:, cols(c % 2, D)], HT[q][:, e, cols(c)],
                                             halves_of(part)[:, e, :],
                                             start=(e == 0 and part is m2_hi), stop=(e == NB - 1 and part is m2_lo))
                    if c % 2:
                        last.then_inc(y2_filled, 1)

            def make_z(i):
                pe.wait_ge(g_hi_ready, 2 * i + 2)
                pe.wait_ge(g_lo_ready, 2 * i + 2)
                for c in range(NB):
                    if isinstance(i, int) and i == 0 and c >= 2:
                        pe.wait_ge(WqkT_f_ready, c - 1)
                    for d in range(DB):
                        for g, w in ((gy_hi, W1T_hi), (gy_hi, W1T_lo), (gy_lo, W1T_hi)):
                            last = pe.matmul(bank[c][:, :], g[:, d, cols(c)], w[:, d, :],
                                             start=(d == 0 and g is gy_hi and w is W1T_hi),
                                             stop=(d == DB - 1 and g is gy_lo))
                    last.then_inc(z_filled, 1)

            def transpose_x1(i):
                pe.wait_ge(x1_ready, i)
                pe.wait_ge(x1_end_ready, i)
                for d in range(DB):
                    for c in range(NB):
                        last = pe.transpose(bank[4 + d][:, cols(c)], x1_of(i)[:, c, cols(d)], ident[:, :])
                    last.then_inc(x1T_filled, 1)

            def make_xmT(i):
                for d in range(DB):
                    pe.wait_ge(x1T_hi_ready, 2 * i - 1 + d)
                    for a in range(DB):
                        for w in (M_hi, M_lo):
                            pe.matmul(bank[2 + a][:, :], w[:, d, cols(a)], x1T_hi[:, d, :],
                                      start=(d == 0 and w is M_hi), stop=False)
                pe.wait_ge(x1T_lo_ready, 2 * i)
                for a in range(DB):
                    for d in range(DB):
                        last = pe.matmul(bank[2 + a][:, :], M_hi[:, d, cols(a)], x1T_lo[:, d, :],
                                         start=False, stop=(d == DB - 1))
                    last.then_inc(xmT_filled, 1)

            def make_v(i):
                for c in range(NB):
                    for s, w in ((x1T_hi, Wv_hi), (x1T_hi, Wv_lo), (x1T_lo, Wv_hi)):
                        for d in range(DB):
                            last = pe.matmul(bank[4 + c // 2][:, cols(c % 2, D)], s[:, d, cols(c)], w[:, d, :],
                                             start=(d == 0 and s is x1T_hi and w is Wv_hi),
                                             stop=(d == DB - 1 and s is x1T_lo))
                    if c % 2:
                        last.then_inc(v_filled, 1)

            def make_S(i, blocks):
                for c in blocks:
                    if c == 0:
                        pe.wait_ge(xmT_hi_ready, 2 * i)
                    if c >= 2:
                        pe.wait_ge(v_ready, 2 * i - 3 + c)
                    for s, r in ((xmT_hi, x1T_hi), (xmT_hi, x1T_lo), (xmT_lo, x1T_hi)):
                        if c == 0 and s is xmT_lo:
                            pe.wait_ge(xmT_lo_ready, 2 * i)
                        for d in range(DB):
                            last = pe.matmul(bank[S_bank[c]][:, :], s[:, d, cols(c)], r[:, d, :],
                                             start=(d == 0 and s is xmT_hi and r is x1T_hi),
                                             stop=(d == DB - 1 and s is xmT_lo))
                    last.then_inc(S_filled, 1)

            def transpose_n1(i):
                for k, to in enumerate(n1T_bank):
                    for c in range(NB):
                        last = pe.transpose(bank[to][:, cols(c)], z[:, c, cols(k)], ident[:, :])
                    last.then_inc(n1T_filled, 1)

            def make_y1(i, c, blocks=range(HB)):
                for k in blocks:
                    if c == 0:
                        pe.wait_ge(n1T_hi_ready, HB * i + k + 1)
                        pe.wait_ge(n1T_lo_ready, HB * i + k + 1)
                    for s, w in ((n1T_hi, W2T_hi), (n1T_hi, W2T_lo), (n1T_lo, W2T_hi)):
                        last = pe.matmul(bank[6 + c // 2][:, cols(c % 2, D)], s[:, k, cols(c)], w[:, k, :],
                                         start=(k == 0 and s is n1T_hi and w is W2T_hi),
                                         stop=(k == HB - 1 and s is n1T_lo))
                if c % 2 and HB - 1 in blocks:
                    last.then_inc(y1_filled, 1)

            def w_to_row(i):
                pe.wait_ge(w_ready, i)
                for c in range(NB):
                    last = pe.transpose(bank[w_bank(i)][0:1, cols(c)], w_masked[:, c:c + 1], ident[:, :])
                last.then_inc(w_filled, 1)

            def p_to_columns(i):
                for c in range(NB):
                    last = pe.transpose(bank[p_bank(i)][:, c:c + 1], p_row[0:1, cols(c)], ident[0:1, 0:1])
                last.then_inc(p_filled, 1)

            def step(i, q, half, prepare, tail, scores):
                nq = 1 - q
                if tail:
                    make_m2(i, nq)
                make_g(i, q, tail)
                if not tail:
                    transpose_Wqk()
                if tail:
                    make_y2(i, nq)
                make_z(i)
                if not tail:
                    set_up_products()
                if prepare:
                    pe.wait_ge(H_bf_ready, NB * i + 2 * NB)
                    if tail:
                        pe.wait_ge(y2_ready, 2 * i)
                    transpose_H(i + 1, 0)
                if tail:
                    transpose_x1(i)
                if prepare:
                    transpose_H(i + 1, 1)
                if tail:
                    pe.wait_ge(z_ready, NB * i + NB)
                    make_xmT(i)
                    if isinstance(i, int) and i < 2:
                        pe.wait_ge(Wv_lo_ready, 1)
                    make_v(i)
                    make_S(i, (0, 1) if scores else (0,))
                pe.wait_ge(n1_ready, i + 1)
                pe.wait_ge(n1_end_ready, i + 1)
                if not tail:
                    pe.wait_ge(W2T_lo_ready, 2)
                elif prepare:
                    pe.wait_ge(HT_ready, NB * i + 2 * NB)
                transpose_n1(i)
                if scores:
                    make_S(i, (2, 3))
                make_y1(i, 0)
                if scores:
                    w_to_row(i)
                make_y1(i, 1)
                make_y1(i, 2)
                make_y1(i, 3, range(HB - 1))
                if scores:
                    pe.wait_ge(p_row_ready, i)
                make_y1(i, 3, range(HB - 1, HB))
                if scores:
                    p_to_columns(i)
                if not tail:
                    pe.wait_ge(M_lo_ready, 1)
                    pe.wait_ge(w2beta_ready, 1)
                if prepare:
                    make_m1(i + 1, nq)

            def last_step():
                make_S(B - 1, (1,))
                make_m2(B, 1)
                make_S(B - 1, (2,))
                make_y2(B, 1)
                make_S(B - 1, (3,))
                pe.wait_ge(scored, NB * (B - 1))
                transpose_x1(B)
                w_to_row(B - 1)
                make_xmT(B)
                pe.wait_ge(p_row_ready, B - 1)
                p_to_columns(B - 1)
                make_v(B)
                pe.wait_ge(p_ready, B - 1)
                make_S(B, (0, 1))
                make_S(B, (2, 3))
                w_to_row(B)
                pe.wait_ge(p_row_ready, B)
                p_to_columns(B)

            steps(pe, step, last_step)

        @block.scalar
        def _(act):
            def copy_HT(q, b, h):
                act.wait_ge(HT_filled, 2 * b + h + 1)
                HT_bank = HT_banks(b)
                for k in range(2):
                    act.activation(HT[q][:, 2 * h + k, :], HT_bank[h][:, cols(k, N)], ACT.Copy,
                                   accum_out=count[q][:, 2 * h + k:2 * h + k + 1]).then_inc(HT_ready, 1)

            def rounded(to, frm, filled, filled_at, ready):
                act.wait_ge(filled, filled_at)
                act.activation(to, frm, ACT.Copy).then_inc(ready, 1)

            def edges_hi(m_hi, q, filled, first_bank, b2, ready):
                for h in range(2):
                    act.wait_ge(filled, b2 + h + 1)
                    for k in range(2):
                        last = act.activation(m_hi[:, h, cols(k, D)], bank[first_bank + h][:, cols(k, D)], ACT.Identity,
                                              scale=Be[q][:, 2 * h + k:2 * h + k + 1], bias=0.0)
                    last.then_inc(ready, 1)

            def normalise(n, to, frm, blocks):
                for k in blocks:
                    last = act.activation(to[:, k, :], frm[:, k, :], ACT.Identity,
                                          scale=rstd[n][:, k:k + 1], bias=shift[n][:, k:k + 1])
                return last

            act.wait_ge(x_in[0], 16)
            act.activation(x_hi[:, :, :], x_raw[0][:, :, :], ACT.Copy).then_inc(x_hi_ready, 1)
            copy_HT(0, 0, 0)
            copy_HT(0, 0, 1)
            act.wait_ge(Be_ready, 1)
            edges_hi(m1_hi, 0, m1_filled, 0, 0, m1_hi_ready)
            for d in range(DB):
                rounded(W1T_hi[:, d, :], bank[2 + d][:, :], W1T_filled, d + 1, W1T_hi_ready)
            act.wait_ge(columns_loaded, 32)
            for h in range(2):
                act.wait_ge(W2T_filled, h + 1)
                for k in range(2 * h, 2 * h + 2):
                    act.activation(W2T_hi[:, k, :], bank[6 + h][:, cols(k % 2, D)], ACT.Identity,
                                   scale=gamma_col[:, k:k + 1], bias=0.0)
                act.activation(W2T_f[:, 2 * h:2 * h + 2, :], halves(bank[6 + h][:, :]), ACT.Copy).then_inc(W2T_f_ready, 1)

            def split_products():
                rounded(M_hi[:, :, :], halves(bank[0][:, :]), M_filled, 1, M_hi_ready)
                act.wait_ge(w2beta_filled, 1)
                act.activation(w2beta[:, 0, :], bank[1][:, 0:D], ACT.Copy)
                act.activation(w2beta[:, 1, :], bank[1][:, 0:D], ACT.Copy).then_inc(w2beta_ready, 1)
                act.wait_ge(Wv_loaded, 16)
                act.activation(Wv_hi[:, :, :], Wv_in, ACT.Copy).then_inc(Wv_hi_ready, 1)

            def x_high(i, q, half):
                act.wait_ge(m1_filled, 2 * i + 2)
                act.wait_ge(x_in[q], 16 * half + 16)
                act.activation(x_hi[:, :, :], x_raw[q][:, :, :], ACT.Copy).then_inc(x_hi_ready, 1)

            def relu(i, c):
                act.wait_ge(z_ready, NB * i + c + 1)
                act.activation(z[:, c, :], z[:, c, :], ACT.Relu).then_inc(relu_ready, 1)

            def y1_hi(i, h):
                act.wait_ge(y1_ready, 2 * i + h + 1)
                act.activation(gy_hi[:, h, :], y1[:, h, :], ACT.Copy).then_inc(y1_hi_ready, 1)


            def make_x1(i):
                act.wait_ge(shift_ready[1], i)
                normalise(1, x1_of(i), y2_of(i), (0, 1)).then_inc(x1_ready, 1)

            def x1T_high(i):
                for d in range(DB):
                    rounded(x1T_hi[:, d, :], bank[4 + d][:, :], x1T_filled, 2 * i - 1 + d, x1T_hi_ready)

            def xmT_high(i):
                for d in range(DB):
                    rounded(xmT_hi[:, d, :], bank[2 + d][:, :], xmT_filled, 2 * i - 1 + d, xmT_hi_ready)

            def make_v(i, h):
                rounded(v[:, h, :], bank[4 + h][:, :], v_filled, 2 * i - 1 + h, v_ready)

            def make_exp(i):
                act.wait_ge(bias_ready, i)
                act.activation(exps[0:1, :], bank[w_bank(i)][0:1, :], ACT.Exp, scale=SCALE, bias=w_bias[0:1, 0:1],
                               accum_out=exp_sum[0:1, 0:1]).then_inc(exp_ready, 1)

            def finish(i):
                act.wait_ge(shift_ready[2], i)
                if not (isinstance(i, int) and i < 2):
                    act.wait_ge(stored, 16 * i - 16)
                normalise(2, result, y2_of(i), (0, 1)).then_inc(result_ready, 1)

            def step(i, q, half, prepare, tail, scores):
                nq = 1 - q
                if tail:
                    edges_hi(m2_hi, nq, m2_filled, 2, 2 * i - 2, m2_hi_ready)
                for d in range(DB):
                    rounded(gy_hi[:, d, :], bank[4 + d][:, :], g_filled, 2 * i + d + 1, g_hi_ready)
                if prepare and tail:
                    x_high(i, nq, half + q)
                if not tail:
                    for h in range(2):
                        rounded(WqkT_f[:, 2 * h:2 * h + 2, :], halves(bank[2 + h][:, :]), WqkT_filled, h + 1, WqkT_f_ready)
                relu(i, 0)
                if tail:
                    make_x1(i)
                relu(i, 1)
                if tail:
                    x1T_high(i)
                relu(i, 2)
                relu(i, 3)
                if prepare and tail:
                    copy_HT(nq, i + 1, 0)
                if tail:
                    xmT_high(i)
                if prepare and tail:
                    copy_HT(nq, i + 1, 1)
                if tail:
                    make_v(i, 0)
                act.wait_ge(shift_ready[0], i + 1)
                normalise(0, z, z, (0, 1)).then_inc(n1_ready, 1)
                if tail:
                    make_v(i, 1)
                else:
                    x_high(0, 1, 0)
                for k, frm in enumerate(n1T_bank):
                    rounded(n1T_hi[:, k, :], bank[frm][:, :], n1T_filled, HB * i + k + 1, n1T_hi_ready)
                if not tail:
                    split_products()
                    copy_HT(1, 1, 0)
                    copy_HT(1, 1, 1)
                if prepare:
                    act.wait_ge(H_bf_ready, NB * i + 2 * NB)
                    act.activation(H[nq][:, :, :], H_bf[:, :, :], ACT.Copy).then_inc(H_ready, 1)
                if scores:
                    make_exp(i)
                y1_hi(i, 0)
                y1_hi(i, 1)
                if prepare:
                    act.wait_ge(Be_ready, i + 2)
                    edges_hi(m1_hi, nq, m1_filled, 0, 2 * i + 2, m1_hi_ready)
                if scores:
                    finish(i)

            def last_step():
                edges_hi(m2_hi, 1, m2_filled, 2, 2 * B - 2, m2_hi_ready)
                make_x1(B)
                x1T_high(B)
                make_exp(B - 1)
                xmT_high(B)
                act.wait_ge(y3_ready, NB * (B - 1))
                make_v(B, 0)
                make_v(B, 1)
                finish(B - 1)
                make_exp(B)
                finish(B)

            steps(act, step, last_step)

        @block.vector
        def _(dve):
            def lo_of(to, frm, hi, hi_ready, hi_at, ready):
                dve.wait_ge(hi_ready, hi_at)
                dve.tensor_tensor(to, frm, hi.bitcast(F32), ALU.subtract).then_inc(ready, 1)

            def edges_lo(m_lo, m_hi, q, first_bank, h, at, hi_ready, ready):
                dve.wait_ge(hi_ready, at)
                for k in range(2):
                    last = dve.scalar_tensor_tensor(m_lo[:, h, cols(k, D)], bank[first_bank + h][:, cols(k, D)],
                                                    Be[q][:, 2 * h + k:2 * h + k + 1],
                                                    m_hi[:, h, cols(k, D)].bitcast(F32), ALU.mult, ALU.subtract)
                last.then_inc(ready, 1)

            def make_H_bf(q, blocks):
                for c in blocks:
                    dve.tensor_scalar(H_bf[:, c, :], adj_raw[q][:, c, :], 0.0, None, ALU.not_equal).then_inc(H_bf_ready, 1)

            def normalise_end(n, to, frm):
                for k in (2, 3):
                    last = dve.tensor_scalar(to[:, k, :], frm[:, k, :], rstd[n][:, k:k + 1], shift[n][:, k:k + 1],
                                             ALU.mult, ALU.add)
                return last

            def guarded_inverse(to, frm, floor, scratch, frm_ready, frm_at, mid_ready, mid_at, ready):
                dve.wait_ge(frm_ready, frm_at)
                dve.tensor_scalar(scratch, frm, floor, None, ALU.max).then_inc(mid_ready, 1)
                dve.wait_ge(mid_ready, mid_at + 1)
                dve.reciprocal(to, scratch).then_inc(mid_ready, 1)
                dve.wait_ge(mid_ready, mid_at + 2)
                dve.scalar_tensor_tensor(to, frm, 0.0, to, ALU.is_gt, ALU.mult).then_inc(ready, 1)

            def make_Be(b, q):
                guarded_inverse(Be[q][:, :], count[q][:, :], 0.5, inv_count[:, :], HT_ready, NB * b + NB,
                                count_inv_ready, 2 * b, Be_ready)

            def sum_degree(q, blocks):
                for c in blocks:
                    dve.scalar_tensor_tensor(unused[:, (c + 2) % NB, :], adj_raw[q][:, c, :], 0.0, row0[q][:, :],
                                             ALU.not_equal, ALU.mult,
                                             accum_out=degree[:, c:c + 1]).then_inc(degree_ready, 1)

            def make_Dn(b, q):
                guarded_inverse(Dn[q][:, :], degree[:, :], TINY, inv_degree[:, :], degree_ready, NB * b + NB,
                                degree_inv_ready, 2 * b, Dn_ready)

            def take_stats(n, frm, k):
                dve.bn_stats(stats[n][:, k, :], frm[:, k, :]).then_inc(stats_ready[n], 1)

            def await_stats(n, b):
                dve.wait_ge(stats_ready[n], 4 * b + 4)

            def take_moments(n):
                for k in range(4):
                    last = dve.bn_aggr(moments[n][:, k, :], stats[n][:, k, :])
                last.then_inc(moments_ready[n], 1)

            def take_shift(n, b):
                dve.wait_ge(rstd_ready[n], b + 1)
                dve.scalar_tensor_tensor(shift[n][:, :], moments[n][:, :, 0], -1.0, rstd[n][:, :],
                                         ALU.mult, ALU.mult).then_inc(shift_ready[n], 1)

            dve.memset(ones[:, :], 1.0).then_inc(ones_ready, 1)
            dve.wait_ge(ident_ready, 1)
            dve.tensor_copy(ident_bf[:, :], ident[:, :]).then_inc(ident_bf_ready, 1)
            for c in range(NB):
                dve.wait_ge(first_adj_in[c], 16)
                make_H_bf(0, (c,))
                dve.tensor_scalar(H[0][:, c, :], adj_raw[0][:, c, :], 0.0, None, ALU.not_equal).then_inc(first_H_ready, 1)
            dve.wait_ge(row0_in[0], 16)
            sum_degree(0, range(2))
            make_Be(0, 0)
            dve.wait_ge(Be_ready, 1)
            for h in range(2):
                edges_lo(m1_lo, m1_hi, 0, 0, h, h + 1, m1_hi_ready, m1_lo_ready)
            for d in range(DB):
                lo_of(W1T_lo[:, d, :], bank[2 + d][:, :], W1T_hi[:, d, :], W1T_hi_ready, d + 1, W1T_lo_ready)
            dve.wait_ge(columns_loaded, 32)
            for h in range(2):
                dve.wait_ge(W2T_f_ready, h + 1)
                for k in range(2 * h, 2 * h + 2):
                    last = dve.scalar_tensor_tensor(W2T_lo[:, k, :], bank[6 + h][:, cols(k % 2, D)],
                                                    gamma_col[:, k:k + 1], W2T_hi[:, k, :].bitcast(F32),
                                                    ALU.mult, ALU.subtract)
                last.then_inc(W2T_lo_ready, 1)

            def spread_beta():
                dve.wait_ge(ones_ready, 1)
                for k in range(HB):
                    last = dve.tensor_scalar(beta_wide[:, k, :], ones[:, :], beta_col[:, k:k + 1], None, ALU.mult)
                last.then_inc(beta_ready, 1)

            def make_y1(i, h):
                dve.wait_ge(y1_filled, 2 * i + h + 1)
                dve.tensor_tensor(y1[:, h, :], bank[6 + h][:, :], w2beta[:, :, :].rearrange("p a d -> p (a d)"),
                                  ALU.add).then_inc(y1_ready, 1)

            def relu_stats(i, c):
                dve.wait_ge(relu_ready, NB * i + c + 1)
                take_stats(0, z, c)


            def make_y2(i, q, h):
                dve.wait_ge(y2_filled, 2 * i - 1 + h)
                for c in range(2 * h, 2 * h + 2):
                    last = dve.scalar_tensor_tensor(y2_of(i)[:, c, :], bank[6 + h][:, cols(c % 2, D)],
                                                    Dn[q][:, c:c + 1], base[:, c, :], ALU.mult, ALU.add)
                last.then_inc(y2_ready, 1)
                dve.wait_ge(y2_ready, 2 * i - 1 + h)
                for c in range(2 * h, 2 * h + 2):
                    take_stats(1, y2_of(i), c)

            def make_x1_end(i):
                take_shift(1, i - 1)
                dve.wait_ge(shift_ready[1], i)
                normalise_end(1, x1_of(i), y2_of(i)).then_inc(x1_end_ready, 1)

            def x1T_low(i):
                for d in range(DB):
                    lo_of(x1T_lo[:, d, :], bank[4 + d][:, :], x1T_hi[:, d, :], x1T_hi_ready, 2 * i - 1 + d, x1T_lo_ready)

            def xmT_low(i, d):
                lo_of(xmT_lo[:, d, :], bank[2 + d][:, :], xmT_hi[:, d, :], xmT_hi_ready, 2 * i - 1 + d, xmT_lo_ready)

            def score(i, q, c):
                dve.wait_ge(S_filled, NB * i - NB + c + 1)
                dve.tensor_tensor_reduce(out=unused[:, c, :], in0=bank[S_bank[c]][:, :], in1=adj_masked[q][:, c, :],
                                         scale=1.0, scalar=0.0, op0=ALU.mult, op1=ALU.add,
                                         accum_out=w_sum[:, c:c + 1]).then_inc(scored, 1)

            def make_w(i):
                dve.wait_ge(scored, NB * i)
                dve.tensor_tensor(w_masked[:, :], w_sum[:, :], mask_col[:, i - 1, :], ALU.mult).then_inc(w_ready, 1)

            def make_max(i):
                dve.wait_ge(w_filled, i)
                dve.tensor_reduce(w_max[:, :], bank[w_bank(i)][0:1, :], AX_X, ALU.max).then_inc(max_ready, 1)
                dve.wait_ge(max_ready, i)
                dve.tensor_scalar(w_bias[:, :], w_max[:, :], -SCALE, None, ALU.mult).then_inc(bias_ready, 1)

            def make_p_row(i):
                dve.wait_ge(exp_ready, i)
                dve.reciprocal(exp_inv[:, :], exp_sum[:, :]).then_inc(exp_inv_ready, 1)
                dve.wait_ge(exp_inv_ready, i)
                dve.tensor_scalar(p_row[:, :], exps[:, :], exp_inv[:, :], None, ALU.mult).then_inc(p_row_ready, 1)

            def make_y3(i):
                dve.wait_ge(p_filled, i)
                dve.tensor_copy(p_col[:, :], bank[p_bank(i)][:, 0:NB]).then_inc(p_ready, 1)
                dve.wait_ge(p_ready, i)
                for c in range(NB):
                    dve.scalar_tensor_tensor(y2_of(i)[:, c, :], v[:, c // 2, cols(c % 2, D)], p_col[:, c:c + 1],
                                             x1_of(i)[:, c, :], ALU.mult, ALU.add).then_inc(y3_ready, 1)

            def y3_stats(i):
                for c in range(NB):
                    dve.wait_ge(y3_ready, NB * i - NB + c + 1)
                    take_stats(2, y2_of(i), c)

            def finish(i):
                take_shift(2, i - 1)
                dve.wait_ge(shift_ready[2], i)
                if not (isinstance(i, int) and i < 2):
                    dve.wait_ge(stored, 16 * i - 16)
                normalise_end(2, result, y2_of(i)).then_inc(result_end_ready, 1)

            def step(i, q, half, prepare, tail, scores):
                nq = 1 - q

                def make_z(c):
                    dve.wait_ge(z_filled, NB * i + c + 1)
                    dve.scalar_tensor_tensor(z[:, c, :], bank[c][:, :], Dn[q][:, c:c + 1], b1_row[:, :],
                                             ALU.mult, ALU.add).then_inc(z_ready, 1)

                if tail:
                    edges_lo(m2_lo, m2_hi, nq, 2, 0, 2 * i - 1, m2_hi_ready, m2_lo_ready)
                    edges_lo(m2_lo, m2_hi, nq, 2, 1, 2 * i, m2_hi_ready, m2_lo_ready)
                if prepare and tail:
                    dve.wait_ge(adj_in[nq], adj_count(half + q, nq))
                    make_H_bf(nq, (0, 1))
                for d in range(DB):
                    lo_of(gy_lo[:, d, :], bank[4 + d][:, :], gy_hi[:, d, :], g_hi_ready, 2 * i + d + 1, g_lo_ready)
                    if not tail:
                        sum_degree(0, (2 + d,))
                if not tail:
                    make_Dn(0, 0)
                    spread_beta()
                if prepare and tail:
                    make_H_bf(nq, (2,))
                if tail:
                    dve.wait_ge(base_ready, i)
                    if not (isinstance(i, int) and i < 2):
                        dve.wait_ge(result_ready, i - 1)
                    make_y2(i, nq, 0)
                    make_y2(i, nq, 1)
                    await_stats(1, i - 1)
                if prepare and tail:
                    make_H_bf(nq, (3,))
                if tail:
                    take_moments(1)
                dve.wait_ge(Dn_ready, i + 1)
                if not tail:
                    dve.wait_ge(rows_loaded, 48)
                make_z(0)
                make_z(1)
                if tail:
                    make_x1_end(i)
                relu_stats(i, 0)
                make_z(2)
                if not tail:
                    relu_stats(i, 1)
                make_z(3)
                if tail:
                    relu_stats(i, 1)
                if tail:
                    x1T_low(i)
                relu_stats(i, 2)
                relu_stats(i, 3)
                await_stats(0, i)
                if tail:
                    xmT_low(i, 0)
                take_moments(0)
                if tail:
                    xmT_low(i, 1)
                else:
                    dve.wait_ge(adj_in[1], 16)
                    make_H_bf(1, range(NB))
                take_shift(0, i)
                dve.wait_ge(shift_ready[0], i + 1)
                normalise_end(0, z, z).then_inc(n1_end_ready, 1)
                if prepare:
                    dve.wait_ge(row0_in[nq], 16 * (half + q) + 16)
                    sum_degree(nq, (0,))
                if tail:
                    dve.wait_ge(masked_ready, NB * i)
                    score(i, nq, 0)
                if prepare:
                    sum_degree(nq, (1,))
                if scores:
                    score(i, nq, 1)
                for k, frm in enumerate(n1T_bank):
                    lo_of(n1T_lo[:, k, :], bank[frm][:, :], n1T_hi[:, k, :], n1T_hi_ready, HB * i + k + 1, n1T_lo_ready)
                if not tail:
                    lo_of(M_lo[:, :, :], halves(bank[0][:, :]), M_hi[:, :, :], M_hi_ready, 1, M_lo_ready)
                    lo_of(Wv_lo[:, :, :], Wv_in, Wv_hi[:, :, :], Wv_hi_ready, 1, Wv_lo_ready)
                    dve.wait_ge(w2beta_ready, 1)
                if scores:
                    if prepare:
                        dve.wait_ge(degree_ready, NB * i + NB + 2)
                    score(i, nq, 2)
                    score(i, nq, 3)
                    make_w(i)
                if prepare:
                    make_Be(i + 1, nq)
                if scores:
                    make_max(i)
                make_y1(i, 0)
                if not prepare:
                    lo_of(gy_lo[:, 0, :], y1[:, 0, :], gy_hi[:, 0, :], y1_hi_ready, 2 * i + 1, y1_lo_ready)
                if scores:
                    make_p_row(i)
                if prepare:
                    sum_degree(nq, (2, 3))
                make_y1(i, 1)
                if not prepare:
                    lo_of(gy_lo[:, 1, :], y1[:, 1, :], gy_hi[:, 1, :], y1_hi_ready, 2 * i + 2, y1_lo_ready)
                if scores:
                    make_y3(i)
                    y3_stats(i)
                    await_stats(2, i - 1)
                if prepare:
                    edges_lo(m1_lo, m1_hi, nq, 0, 0, 2 * i + 3, m1_hi_ready, m1_lo_ready)
                if scores:
                    take_moments(2)
                if prepare:
                    edges_lo(m1_lo, m1_hi, nq, 0, 1, 2 * i + 4, m1_hi_ready, m1_lo_ready)
                    make_Dn(i + 1, nq)
                if scores:
                    finish(i)

            def last_step():
                dve.wait_ge(masked_ready, NB * B)
                score(B - 1, 0, 1)
                edges_lo(m2_lo, m2_hi, 1, 2, 0, 2 * B - 1, m2_hi_ready, m2_lo_ready)
                edges_lo(m2_lo, m2_hi, 1, 2, 1, 2 * B, m2_hi_ready, m2_lo_ready)
                score(B - 1, 0, 2)
                dve.wait_ge(base_ready, B)
                make_y2(B, 1, 0)
                make_y2(B, 1, 1)
                await_stats(1, B - 1)
                take_moments(1)
                score(B - 1, 0, 3)
                make_x1_end(B)
                make_w(B - 1)
                x1T_low(B)
                make_max(B - 1)
                make_p_row(B - 1)
                xmT_low(B, 0)
                xmT_low(B, 1)
                make_y3(B - 1)
                y3_stats(B - 1)
                await_stats(2, B - 2)
                take_moments(2)
                score(B, 1, 0)
                score(B, 1, 1)
                finish(B - 1)
                score(B, 1, 2)
                score(B, 1, 3)
                make_w(B)
                make_max(B)
                make_p_row(B)
                make_y3(B)
                y3_stats(B)
                await_stats(2, B - 1)
                take_moments(2)
                finish(B)

            steps(dve, step, last_step)

        @block.gpsimd
        def _(pool):
            def x_low(b, q):
                pool.wait_ge(x_hi_ready, b + 1)
                pool.tensor_tensor(x_lo[:, :, :], x_raw[q][:, :, :], x_hi[:, :, :].bitcast(F32),
                                   ALU.subtract).then_inc(x_lo_ready, 1)

            def inverse_std(n, b):
                pool.wait_ge(moments_ready[n], b + 1)
                pool.tensor_tensor(varp[n][:, :], moments[n][:, :, 1], eps_col[:, :], ALU.add)\
                    .then_inc(varp_ready[n], 1)
                pool.wait_ge(varp_ready[n], b + 1)
                pool.tensor_tensor(rstd[n][:, :], varp[n][:, :], minus_half[:, :], ALU.pow).then_inc(rstd_ready[n], 1)

            pool.memset(minus_half[:, :], -0.5).then_inc(half_ready, 1)
            pool.memset(eps_col[:, :], EPS).then_inc(half_ready, 1)
            pool.memset(ident[:, :], 0.0).then_inc(ident_zero, 1)
            pool.wait_ge(ident_zero, 1)
            pool.affine_select(out=ident[:, :], in_=ident[:, :], compare_op=ALU.not_equal, fill=1.0, base=0,
                               pattern=[[-1, P]], channel_multiplier=1).then_inc(ident_ready, 1)
            x_low(0, 0)
            pool.wait_ge(half_ready, 2)

            def y1_low(i, h):
                pool.wait_ge(y1_hi_ready, 2 * i + h + 1)
                pool.tensor_tensor(gy_lo[:, h, :], y1[:, h, :], gy_hi[:, h, :].bitcast(F32),
                                   ALU.subtract).then_inc(y1_lo_ready, 1)

            def step(i, q, half, prepare, tail, scores):
                nq = 1 - q
                pool.wait_ge(maskrow_in[q], 16 * half + 16)
                if not tail:
                    for c in range(NB):
                        pool.wait_ge(first_adj_in[c], 16)
                else:
                    pool.wait_ge(adj_in[q], adj_count(half, q))
                if not (isinstance(i, int) and i < 2):
                    pool.wait_ge(scored, NB * i - NB)
                for c in range(NB):
                    pool.tensor_tensor(adj_masked[q][:, c, :].rearrange("p (k n) -> p k n", k=NB),
                                       adj_raw[q][:, c, :].rearrange("p (n k) -> p k n", k=NB),
                                       maskrow[q][:, :].rearrange("p (n k) -> p k n", k=NB),
                                       ALU.mult).then_inc(masked_ready, 1)
                if not tail:
                    inverse_std(0, 0)
                if prepare:
                    x_low(i + 1, nq)
                if tail:
                    inverse_std(1, i - 1)
                    pool.wait_ge(y2_ready, 2 * i)
                else:
                    pool.wait_ge(rows_loaded, 48)
                pool.tensor_tensor(base[:, :, :], x_raw[q][:, :, :], x_raw[q][:, :, :], ALU.add)\
                    .then_inc(twice_ready, 1)
                pool.wait_ge(twice_ready, i + 1)
                pool.tensor_tensor(base[:, :, :], base[:, :, :],
                                   b2_row[:, :].rearrange("p (a d) -> p a d", a=1).to_broadcast([P, NB, D]),
                                   ALU.add).then_inc(base_ready, 1)
                if tail:
                    inverse_std(0, i)
                if prepare:
                    y1_low(i, 0)
                    y1_low(i, 1)
                if scores:
                    inverse_std(2, i - 1)

            def last_step():
                inverse_std(1, B - 1)
                inverse_std(2, B - 2)
                inverse_std(2, B - 1)

            steps(pool, step, last_step)


_INS = ['x', 'adj', 'nodemask', 'L0_gnn_W1', 'L0_gnn_b1', 'L0_gnn_gamma', 'L0_gnn_beta', 'L0_gnn_W2', 'L0_gnn_b2',
        'L1_gnn_Wqk', 'L1_gnn_Wv']


def kernel(**inputs):
    import numpy as _np
    import concourse.bacc as _bacc
    from concourse import mybir as _mybir
    from concourse.bass_utils import run_bass_kernel_spmd as _run

    nc = _bacc.Bacc("TRN2", target_bir_lowering=False, num_devices=1)
    arrays, args = {}, []
    for name in _INS:
        a = _np.ascontiguousarray(inputs[name])
        arrays[f"in_{name}_dram"] = a
        args.append(nc.dram_tensor(f"in_{name}_dram", a.shape, _mybir.dt.from_np(a.dtype), kind="ExternalInput").ap())
    shape = inputs['x'].shape
    args.append(nc.dram_tensor("out_dram", shape, _mybir.dt.from_np(_np.dtype('float32')), kind="ExternalOutput").ap())
    graph_kernel(nc, *args)
    r = _run(nc, [arrays], core_ids=[0])
    return r.results[0]["out_dram"]
```
